# Optimizing a Trainium2 kernel written in Bass

```python
import numpy as np
import jax
import jax.numpy as jnp

def _softmax(x, axis=-1):
    return jax.nn.softmax(x, axis=axis)

def _gelu(x):
    return jax.nn.gelu(x, approximate=True)

def _silu(x):
    return jax.nn.silu(x)

def _sigmoid(x):
    return jax.nn.sigmoid(x)

def _layernorm(x, axis=-1, eps=1e-05):
    m = jnp.mean(x, axis=axis, keepdims=True)
    v = jnp.var(x, axis=axis, keepdims=True)
    return (x - m) / jnp.sqrt(v + eps)

def _scatter_add(tgt, idx, src, axis=0):
    return tgt.at[idx].add(src)

def _segment_sum(src, seg, n):
    return jax.ops.segment_sum(src, seg, n)
kernel_name = 'mk_prb_d1_jaxref_r8_f0dc4b'

def setup_inputs(seed: int=0):
    np.random.seed(seed)
    _w = jnp.asarray

    def _L0_attn_setup():
        import math
        import jax, jax.numpy as jnp
        import numpy as np
        EMBED_DIM = 128
        NUM_HEADS = 16
        FACTOR = 5
        key = jax.random.key(seed)
        kx, kw, kb, kow, kob = jax.random.split(key, 5)
        B, S, E = (8, 512, EMBED_DIM)
        scale = 1.0 / math.sqrt(E)
        x = jax.random.normal(kx, (B, S, E), dtype=jnp.float32)
        in_proj_w = jax.random.uniform(kw, (3 * E, E), dtype=jnp.float32, minval=-scale, maxval=scale)
        in_proj_b = jnp.zeros((3 * E,), dtype=jnp.float32)
        out_w = jax.random.uniform(kow, (E, E), dtype=jnp.float32, minval=-scale, maxval=scale)
        out_b = jnp.zeros((E,), dtype=jnp.float32)
        return {'x': x, 'in_proj_w': in_proj_w, 'in_proj_b': in_proj_b, 'out_w': out_w, 'out_b': out_b}
    _L0_attn_in = _L0_attn_setup()

    def _L0_ffn_setup():
        import jax, jax.numpy as jnp
        import numpy as np
        L, E, H, F, K = (4, 4, 128, 512, 2)
        B, S = (4, 256)
        EPS = 1e-05

        def _moe_layer(x, rw, rb, g, b, w1, b1, w2, b2):
            logits = jnp.einsum('bsh,he->bse', x, rw) + rb
            probs = jax.nn.softmax(logits, axis=-1)
            vals, idx = jax.lax.top_k(probs, K)
            vals = vals / vals.sum(axis=-1, keepdims=True)
            mu = x.mean(axis=-1, keepdims=True)
            xc = x - mu
            xhat = xc * jax.lax.rsqrt((xc * xc).mean(axis=-1, keepdims=True) + EPS)
            xe = xhat[None] * g[:, None, None, :] + b[:, None, None, :]
            h = jax.nn.gelu(jnp.einsum('ebsh,ehf->ebsf', xe, w1) + b1[:, None, None, :], approximate=False)
            y = jnp.einsum('ebsf,efh->ebsh', h, w2) + b2[:, None, None, :]
            expert_out = x[None] + y
            comb = jnp.einsum('bsk,bske->bse', vals, jax.nn.one_hot(idx, E, dtype=x.dtype))
            return jnp.einsum('bse,ebsh->bsh', comb, expert_out)
        key = jax.random.key(seed)
        ks = jax.random.split(key, 4)
        return {'hidden_states': jax.random.normal(ks[0], (B, S, H), jnp.float32), 'router_w': 0.02 * jax.random.normal(ks[1], (L, H, E), jnp.float32), 'router_b': jnp.zeros((L, E), jnp.float32), 'ln_g': jnp.ones((L, E, H), jnp.float32), 'ln_b': jnp.zeros((L, E, H), jnp.float32), 'w1': 0.02 * jax.random.normal(ks[2], (L, E, H, F), jnp.float32), 'b1': jnp.zeros((L, E, F), jnp.float32), 'w2': 0.02 * jax.random.normal(ks[3], (L, E, F, H), jnp.float32), 'b2': jnp.zeros((L, E, H), jnp.float32)}
    _L0_ffn_in = _L0_ffn_setup()
    _d = {'L0_attn_x': _L0_attn_in['x'], 'L0_attn_in_proj_w': _L0_attn_in['in_proj_w'], 'L0_attn_in_proj_b': _L0_attn_in['in_proj_b'], 'L0_attn_out_w': _L0_attn_in['out_w'], 'L0_attn_out_b': _L0_attn_in['out_b'], 'L0_ffn_router_w': _L0_ffn_in['router_w'], 'L0_ffn_router_b': _L0_ffn_in['router_b'], 'L0_ffn_ln_g': _L0_ffn_in['ln_g'], 'L0_ffn_ln_b': _L0_ffn_in['ln_b'], 'L0_ffn_w1': _L0_ffn_in['w1'], 'L0_ffn_b1': _L0_ffn_in['b1'], 'L0_ffn_w2': _L0_ffn_in['w2'], 'L0_ffn_b2': _L0_ffn_in['b2']}
    _x0 = _d['L0_attn_x']
    _d['L0_attn_x'] = jax.random.normal(jax.random.fold_in(jax.random.key(seed), 1), (16, 256, 128), dtype=_x0.dtype)
    del _x0
    return _d

def reference(L0_attn_x, L0_attn_in_proj_w, L0_attn_in_proj_b, L0_attn_out_w, L0_attn_out_b, L0_ffn_router_w, L0_ffn_router_b, L0_ffn_ln_g, L0_ffn_ln_b, L0_ffn_w1, L0_ffn_b1, L0_ffn_w2, L0_ffn_b2):

    def _L0_attn_ref(x, in_proj_w, in_proj_b, out_w, out_b):
        import math
        import jax, jax.numpy as jnp
        import numpy as np
        EMBED_DIM = 128
        NUM_HEADS = 16
        FACTOR = 5
        B, S, E = x.shape
        H = NUM_HEADS
        hd = E // H
        k = max(1, int(FACTOR * math.log(S + 1)))
        k = min(k, S)
        energy = jnp.linalg.norm(x, axis=-1)
        _, topk_idx = jax.lax.top_k(energy, k)
        q_tok = jnp.take_along_axis(x, topk_idx[..., None], axis=1)
        Wq, Wk, Wv = jnp.split(in_proj_w, 3, axis=0)
        bq, bk, bv = jnp.split(in_proj_b, 3, axis=0)
        q = (q_tok @ Wq.T + bq).reshape(B, k, H, hd)
        kk = (x @ Wk.T + bk).reshape(B, S, H, hd)
        v = (x @ Wv.T + bv).reshape(B, S, H, hd)
        scores = jnp.einsum('bqhd,bshd->bhqs', q, kk) / math.sqrt(hd)
        attn = jax.nn.softmax(scores, axis=-1)
        ctx = jnp.einsum('bhqs,bshd->bqhd', attn, v).reshape(B, k, E)
        out_sel = ctx @ out_w.T + out_b
        default = jnp.mean(x, axis=1)
        result = jnp.broadcast_to(default[:, None, :], (B, S, E))
        batch_ar = jnp.arange(B)[:, None]
        result = result.at[batch_ar, topk_idx].set(out_sel)
        return result

    def _L0_ffn_ref(hidden_states, router_w, router_b, ln_g, ln_b, w1, b1, w2, b2):
        import jax, jax.numpy as jnp
        import numpy as np
        L, E, H, F, K = (4, 4, 128, 512, 2)
        B, S = (4, 256)
        EPS = 1e-05

        def _moe_layer(x, rw, rb, g, b, w1, b1, w2, b2):
            logits = jnp.einsum('bsh,he->bse', x, rw) + rb
            probs = jax.nn.softmax(logits, axis=-1)
            vals, idx = jax.lax.top_k(probs, K)
            vals = vals / vals.sum(axis=-1, keepdims=True)
            mu = x.mean(axis=-1, keepdims=True)
            xc = x - mu
            xhat = xc * jax.lax.rsqrt((xc * xc).mean(axis=-1, keepdims=True) + EPS)
            xe = xhat[None] * g[:, None, None, :] + b[:, None, None, :]
            h = jax.nn.gelu(jnp.einsum('ebsh,ehf->ebsf', xe, w1) + b1[:, None, None, :], approximate=False)
            y = jnp.einsum('ebsf,efh->ebsh', h, w2) + b2[:, None, None, :]
            expert_out = x[None] + y
            comb = jnp.einsum('bsk,bske->bse', vals, jax.nn.one_hot(idx, E, dtype=x.dtype))
            return jnp.einsum('bse,ebsh->bsh', comb, expert_out)
        x = hidden_states
        for l in range(L):
            x = _moe_layer(x, router_w[l], router_b[l], ln_g[l], ln_b[l], w1[l], b1[l], w2[l], b2[l])
        return x
    x = L0_attn_x
    xn = _layernorm(x, axis=-1)
    x = x + _L0_attn_ref(xn, L0_attn_in_proj_w, L0_attn_in_proj_b, L0_attn_out_w, L0_attn_out_b) + _L0_ffn_ref(xn, L0_ffn_router_w, L0_ffn_router_b, L0_ffn_ln_g, L0_ffn_ln_b, L0_ffn_w1, L0_ffn_b1, L0_ffn_w2, L0_ffn_b2)
    return x

_drawn_inputs = setup_inputs


def setup_inputs(seed=0):
    import zlib

    import numpy as np

    out = dict(_drawn_inputs(seed))
    spreads = {'L0_attn_in_proj_b': (0.0, 0.8),
     'L0_attn_out_b': (0.0, 1.456),
     'L0_ffn_router_b': (0.0, 0.382),
     'L0_ffn_ln_g': (1.0, 0.6),
     'L0_ffn_ln_b': (0.0, 2.0),
     'L0_ffn_b1': (0.0, 1.211),
     'L0_ffn_b2': (0.0, 0.304)}
    factors = {'L0_attn_in_proj_w': 8.0, 'L0_attn_out_w': 6.29}
    for name, (base, spread) in spreads.items():
        noise = np.random.default_rng([zlib.crc32(name.encode()), seed]).standard_normal(out[name].shape)
        drawn = base * np.exp(spread * noise) if base else spread * noise
        out[name] = jnp.asarray(drawn.astype(out[name].dtype))
    for name, factor in factors.items():
        out[name] = (out[name] * factor).astype(out[name].dtype)
    return out
```

```python
import concourse.bass as bass
from concourse import mybir
from contextlib import ExitStack


def attention_and_experts_kernel(
    nc: bass.Bass,
    x_dram: bass.AP,
    in_proj_w: bass.AP,
    in_proj_b: bass.AP,
    out_w: bass.AP,
    out_b: bass.AP,
    router_w: bass.AP,
    router_b: bass.AP,
    ln_g: bass.AP,
    ln_b: bass.AP,
    w1_dram: bass.AP,
    b1_dram: bass.AP,
    w2_dram: bass.AP,
    b2_dram: bass.AP,
    out_dram: bass.AP,
):
    fp32 = mybir.dt.float32
    fp32r = mybir.dt.float32r
    u32 = mybir.dt.uint32
    ALU = mybir.AluOpType
    ACT = mybir.ActivationFunctionType
    X = mybir.AxisListType.X

    B, S, D = x_dram.shape
    P = 128
    TB = S // P
    NT = B * TB
    L, E, _, F = w1_dram.shape
    FC = F // P
    GT = 4
    NG = NT // GT
    GN = GT * P
    EPS = 1e-5
    NH = 16
    HD = D // NH
    TOP = 27
    SEL = TOP + 1
    CH = 4
    HC = NH // CH
    QC = HC * TOP
    SCALE = float(HD) ** -0.5
    HIGH = 0xFFFFF000
    K_TOP = 2

    x_v = x_dram.rearrange("b (t p) h -> p (b t) h", p=P)
    out_v = out_dram.rearrange("b (t p) h -> p (b t) h", p=P)

    ctx = ExitStack()
    with ctx:
        def sb(name, shape, dt=fp32):
            return ctx.enter_context(nc.sbuf_tensor(name, shape, dt))

        def sem(name):
            return ctx.enter_context(nc.semaphore(name))

        x_in = sb("x_in", [P, NT, D])
        xn_all = sb("xn_all", [P, NT, D])
        state = sb("state", [P, NT, D])
        raw = sb("raw", [P, L * E * 2 * F])
        w1_raw = raw[:, 0:L * E * F].rearrange("p (m f) -> p m f", f=F)
        w2_raw = raw[:, L * E * F:].rearrange("p (m c h) -> p m c h", c=FC, h=D)
        w1_hi = sb("w1_hi", [P, E, F], fp32r)
        w1_lo = sb("w1_lo", [P, E, F], fp32r)
        w1_gs = [sb(f"w1_g{i}", [P, F]) for i in range(2)]
        w2 = sb("w2", [P, E, FC, D])
        NB1 = L * E * FC
        COL_G, COL_B, COL_B1, COL_QKV = 0, L * E, 2 * L * E, 2 * L * E + NB1
        NCOL = COL_QKV + 3
        rows = sb("rows", [P, P])
        cols = sb("cols", [P, NCOL])
        bias1 = sb("bias1", [P, NB1])
        bias_l = sb("bias_l", [P, E * FC])
        LE1 = (L + 1) * E
        rw = sb("rw", [P, LE1])
        rw_hi = sb("rw_hi", [P, LE1], fp32r)
        rw_lo = sb("rw_lo", [P, LE1], fp32r)
        rb = sb("rb", [P, LE1])
        rw_sum = sb("rw_sum", [P, LE1])
        b2 = sb("b2", [E, L + 1, D])
        proj = sb("proj", [P, 4, D])
        projT = sb("projT", [P, 4, D])
        ob = sb("ob", [1, D])
        ident = sb("ident", [P, P])
        ones = sb("ones", [P, P])
        before4 = sb("before4", [P, E, E])
        before = sb("before", [P, TB, S])
        slot = sb("slot", [P, SEL])
        heads = sb("heads", [P, NH, TOP])
        mean_row = sb("mean_row", [P, SEL])
        top_row = sb("top_row", [1, SEL])
        half = sb("half", [P, NT])
        grp = [sb(f"grp{i}", [P, GT, D]) for i in range(2)]
        xhat = sb("xhat", [P, GT, D])
        xT_hi = [sb(f"xT_hi{i}", [P, GN], fp32r) for i in range(2)]
        xT_lo = [sb(f"xT_lo{i}", [P, GN], fp32r) for i in range(2)]
        hid = [sb(f"hid{i}", [P, FC, GN]) for i in range(2)]
        stats = sb("stats", [P, GT, 6])
        mv = sb("mv", [P, GT, 2])
        ve = sb("ve", [P, GT])
        sd = sb("sd", [P, GT])
        rsd = sb("rsd", [P, GT])
        lg = sb("lg", [P, GT, E])
        lg_a = sb("lg_a", [P, GT, E])
        arg = sb("arg", [P, GT, E])
        th = sb("th", [P, GT, E])
        cmp_gt = sb("cmp_gt", [P, GT, E, E])
        cmp_eq = sb("cmp_eq", [P, GT, E, E])
        place = sb("place", [P, GT, E])
        chosen = sb("chosen", [P, GT, E])
        two = sb("two", [P, GT])
        comb = [sb(f"comb{i}", [P, GT, E]) for i in range(2)]
        combT = sb("combT", [E, GN])
        lane = sb("lane", [P, GT, 16])
        lane8 = sb("lane8", [P, GT, 2, 4])
        lane4 = sb("lane4", [P, GT, 4])
        lane2 = sb("lane2", [P, GT, 2])
        mean = sb("mean", [P, GT])
        dev = sb("dev", [P, GT, D])
        q0 = sb("q0", [P, GT, D])
        q_hi = sb("q_hi", [P, GT, D])
        q_lo = sb("q_lo", [P, GT, D])
        rem = sb("rem", [P, GT, D])
        xn = sb("xn", [P, GT, D])
        win = sb("win", [P, GT, 4])
        vsum = sb("vsum", [P, GT])
        var = sb("var", [P, GT])
        sqs = [sb(f"sqs{i}", [P, NT]) for i in range(8)]
        norm2 = sb("norm2", [P, NT])
        norm = sb("norm", [P, NT])
        sd_x = sb("sd_x", [P, GT])
        sd_hi = sb("sd_hi", [P, GT])
        sd_lo = sb("sd_lo", [P, GT])
        inv = sb("inv", [P, GT])
        ninv = sb("ninv", [P, GT])
        root0 = sb("root0", [P, NT])
        at = [0]

        def carve(n):
            at[0] += n
            return raw[:, at[0] - n:at[0]]

        xb = [carve(TB * D).rearrange("p (t h) -> p t h", h=D) for _ in range(2)]
        eb = [carve(TB * P).rearrange("p (t h) -> p t h", h=P) for _ in range(2)]
        ecol = [carve(TB) for _ in range(2)]
        xbT = carve(S)
        kT = [carve(S) for _ in range(2)]
        v = [carve(TB * D).rearrange("p (t h) -> p t h", h=D) for _ in range(2)]
        gt_out = carve(S)
        eq_out = carve(S)
        n_gt = carve(TB)
        n_eq = carve(TB)
        rank = carve(TB)
        onehot = carve(TB * SEL).rearrange("p (t q) -> p t q", q=SEL)
        onehotT = [carve(S) for _ in range(2)]
        xqT = carve(SEL)
        qT = carve(SEL)
        qbd = [carve(NH * TOP).rearrange("p (h q) -> p h q", q=TOP) for _ in range(2)]
        prob = carve(CH * S).rearrange("p (c s) -> p c s", s=S)
        mx = carve(CH)
        nmx = carve(CH)
        den = carve(CH)
        rden = carve(CH)
        pT = carve(TB * NH * TOP).rearrange("p (t r) -> p t r", t=TB)
        picked = carve(NH * TOP).rearrange("p (h q) -> p h q", q=TOP)
        cx = carve(TOP)
        ctxT = carve(SEL)
        res = carve(D)
        sum1 = carve(TB * D).rearrange("p (t h) -> p t h", h=D)
        out_sb = [carve(TB * D).rearrange("p (t h) -> p t h", h=D) for _ in range(2)]
        bank = [ctx.enter_context(nc.psum_tensor(f"bank{i}", [P, GN], fp32)) for i in range(8)]
        h_ps = bank[0:4]
        y_ps = bank[4:6]
        t_ps, m_ps = bank[6], bank[7]

        ld_x = [sem(f"ld_x{g}") for g in range(NG)]
        ld_rows, ld_w1, ld_w2 = sem("ld_rows"), sem("ld_w1"), [sem(f"ld_w2_{l}") for l in range(L)]
        ld_proj, ld_small = sem("ld_proj"), sem("ld_small")
        pool_seq = sem("pool_seq")
        pool_const = sem("pool_const")
        pool_w2 = sem("pool_w2")
        pool_bias = sem("pool_bias")
        pool_alone = sem("pool_alone")
        pool_grp = sem("pool_grp")
        pool_sd = sem("pool_sd")
        pool_root = sem("pool_root")
        pool_xn = sem("pool_xn")
        pool_store = sem("pool_store")
        dve_seq = sem("dve_seq")
        dve_setup = sem("dve_setup")
        dve_b1 = sem("dve_b1")
        dve_w1 = sem("dve_w1")
        dve_var = sem("dve_var")
        dve_xhat = sem("dve_xhat")
        dve_xT = sem("dve_xT")
        dve_arg = sem("dve_arg")
        dve_comb = sem("dve_comb")
        dve_combT = sem("dve_combT")
        dve_z = sem("dve_z")
        dve_y = sem("dve_y")
        dve_exvar = sem("dve_exvar")
        dve_xn = sem("dve_xn")
        pe_setup = sem("pe_setup")
        pe_b1 = sem("pe_b1")
        pe_xT = sem("pe_xT")
        pe_lg = sem("pe_lg")
        pe_combT = sem("pe_combT")
        pe_z = sem("pe_z")
        pe_h = [sem(f"pe_h{f}") for f in range(FC)]
        pe_y = sem("pe_y")
        act_h = [sem(f"act_h{f}") for f in range(FC)]
        act_th = sem("act_th")
        a_in, a_rowE, a_xbT, a_kv, a_xq, a_ohT, a_q = (sem(f"a_{n}") for n in "in rowE xbT kv xq ohT q".split())
        a_xbTs, a_kTs, a_vs, a_oh, a_xqs, a_ohTs, a_qbd = (
            sem(f"a_{n}") for n in "xbTs kTs vs oh xqs ohTs qbd".split())
        a_sc, a_mx, a_exp, a_pr, a_pt, a_pt0, a_pt1 = (sem(f"a_{n}") for n in "sc mx exp pr pt pt0 pt1".split())
        a_cx, a_cxs, a_res, a_ress, a_out, a_outs, a_norm = (
            sem(f"a_{n}") for n in "cx cxs res ress out outs norm".split())
        a_root = sem("a_root")
        st_out = [sem(f"st_out{i}") for i in range(2)]

        class Own:

            def __init__(self, eng, s):
                self.eng, self.s, self.n = eng, s, 0

            def __call__(self, ins, instead=None):
                if instead is not None:
                    ins.then_inc(instead, 1)
                else:
                    self.n += 1
                    ins.then_inc(self.s, 1)
                return self.n

            def wait(self, n=None):
                n = self.n if n is None else n
                if n > 0:
                    self.eng.wait_ge(self.s, n)

            def clear(self):
                self.wait()
                self.eng.sem_clear(self.s)
                self.n = 0

        block = ctx.enter_context(nc.Block())

        @block.sync
        def _(sp):
            def load_x(g):
                sp.dma_start(x_in[:, g * GT:(g + 1) * GT, :],
                             x_v[:, g * GT:(g + 1) * GT, :]).then_inc(ld_x[g], 16)

            load_x(0)
            sp.dma_start(rows[COL_G:COL_B, :], ln_g.rearrange("l e h -> (l e) h")).then_inc(ld_rows, 16)
            sp.dma_start(rows[COL_B:COL_B1, :], ln_b.rearrange("l e h -> (l e) h")).then_inc(ld_rows, 16)
            sp.dma_start(rows[COL_B1:COL_QKV, :],
                         b1_dram.rearrange("l e (c p) -> (l e c) p", p=P)).then_inc(ld_rows, 16)
            sp.dma_start(rows[COL_QKV:NCOL, :],
                         in_proj_b.rearrange("(c p) -> c p", p=P)).then_inc(ld_rows, 16)
            load_x(1)
            for l in range(L):
                sp.dma_start(w1_raw[:, l * E:(l + 1) * E, :],
                             w1_dram[l].rearrange("e p f -> p e f")).then_inc(ld_w1, 16)
            for i in range(2):
                sp.wait_ge(st_out[i], 16 * B // 2 + 16)

        @block.scalar
        def _(act):
            act.dma_start(rw[:, 0:L * E], router_w.rearrange("l h e -> h l e")).then_inc(ld_small, 16)
            act.dma_start(rb[:, 0:L * E],
                          router_b.rearrange("l e -> (l e)").partition_broadcast(P)).then_inc(ld_small, 16)
            act.dma_start(b2[:, 0:L, :], b2_dram.rearrange("l e h -> e l h")).then_inc(ld_small, 16)
            act.dma_start(ob[:], out_b.unsqueeze(0)).then_inc(ld_small, 16)
            act.dma_start(proj[:, 0:3, :], in_proj_w.rearrange("(c p) h -> p c h", p=P)).then_inc(ld_proj, 16)
            act.dma_start(proj[:, 3, :], out_w).then_inc(ld_proj, 16)
            for g in range(2, NG):
                act.dma_start(x_in[:, g * GT:(g + 1) * GT, :],
                              x_v[:, g * GT:(g + 1) * GT, :]).then_inc(ld_x[g], 16)
            for l in range(L):
                act.dma_start(w2_raw[:, l * E:(l + 1) * E, :, :],
                              w2_dram[l].rearrange("e (c p) h -> p e c h", p=P)).then_inc(ld_w2[l], 16)
            for f in range(FC):
                act.sem_inc(act_h[f], 1)
            for i in range(2):
                act.sem_inc(st_out[i], 16)

            def weigh(n2):
                act.wait_ge(dve_arg, n2)
                nc.scalar.activation(th[:], arg[:], ACT.Tanh).then_inc(act_th, 1)

            weigh(1)
            with act.Fori(0, L) as l:
                act.wait_ge(pool_bias, nc.scalar.snap(l + 1))
                with act.Fori(0, NG // 2) as i:
                    for s in range(2):
                        n = l * NG + i * 2 + s
                        c = [nc.scalar.snap(n * E + k) for k in range(1, E + 1)]
                        n2 = nc.scalar.snap(n + 2)
                        for e in range(E):
                            for f in range(FC):
                                if f == 0:
                                    act.wait_ge(pe_y, c[e])
                                act.wait_ge(pe_h[f], c[e])
                                nc.scalar.activation(
                                    hid[e % 2][:, f, :], h_ps[f][:], ACT.Gelu,
                                    bias=bias_l[:, e * FC + f:e * FC + f + 1],
                                ).then_inc(act_h[f], 1)
                        weigh(n2)

            def keep_keys(b1):
                act.wait_ge(a_xbT, b1)
                nc.scalar.copy(xbT[:], bank[1][:, 0:S]).then_inc(a_xbTs, 1)

            def keep_kv(b1, s):
                act.wait_ge(a_kv, b1)
                nc.scalar.activation(kT[s][:], bank[3][:, 0:S], ACT.Identity,
                                     bias=cols[:, COL_QKV + 1:COL_QKV + 2]).then_inc(a_kTs, 1)
                nc.scalar.copy(v[s][:].rearrange("p t h -> p (t h)"), bank[3][:, S:2 * S]).then_inc(a_vs, 1)

            keep_keys(1)
            keep_kv(1, 0)
            with act.Fori(0, B // 2) as i:
                for s in range(2):
                    b1 = nc.scalar.snap(i * 2 + (s + 1))
                    b2_ = nc.scalar.snap(i * 2 + (s + 2))
                    act.wait_ge(a_mx, b1)
                    for c in range(CH):
                        ins = nc.scalar.activation(
                            prob[0:QC, c, :], bank[4 + c // 2][0:QC, (c % 2) * S:(c % 2 + 1) * S], ACT.Exp,
                            bias=nmx[0:QC, c:c + 1], scale=SCALE, accum_out=den[0:QC, c:c + 1])
                    ins.then_inc(a_exp, 1)
                    keep_keys(b2_)
                    keep_kv(b2_, 1 - s)
                    act.wait_ge(a_pt, b1)
                    nc.scalar.copy(pT[:, 1, :], bank[7][:, 0:NH * TOP]).then_inc(a_pt1, 1)
                    act.wait_ge(a_res, b2_)
                    nc.scalar.copy(res[0:SEL, :], bank[5][0:SEL, 0:D]).then_inc(a_ress, 1)
                    act.wait_ge(a_outs, b1)
                    act.dma_start(out_v[:, bass.ds(i * (2 * TB) + s * TB, TB), :],
                                  out_sb[s][:]).then_inc(st_out[s], 16)

        @block.gpsimd
        def _(pool):
            own = Own(pool, pool_seq)

            def select(t, compare, fill, base, pattern, mult):
                return own(nc.gpsimd.affine_select(out=t, in_=t, compare_op=compare, fill=fill, base=base,
                                                   pattern=pattern, channel_multiplier=mult))

            own(nc.gpsimd.memset(ident[:], 0.0))
            own(nc.gpsimd.memset(ones[:], 1.0))
            own(nc.gpsimd.memset(before4[:], 0.0))
            own(nc.gpsimd.memset(before[:], 0.0))
            own(nc.gpsimd.memset(heads[:], 1.0))
            own(nc.gpsimd.memset(mean_row[:], 0.0))
            own(nc.gpsimd.memset(top_row[:], 1.0))
            own(nc.gpsimd.memset(half[:], 0.5))
            own(nc.gpsimd.memset(rw[:, L * E:], 0.0))
            own(nc.gpsimd.memset(rb[:, L * E:], 0.0))
            own(nc.gpsimd.memset(b2[:, L, :], 0.0))
            own(nc.gpsimd.iota(slot[:], pattern=[[1, SEL]], base=0, channel_multiplier=0,
                               allow_small_or_imprecise_dtypes=True))
            own.wait()
            select(ident[:], ALU.not_equal, 1.0, 0, [[-1, P]], 1)
            select(before4[:], ALU.is_ge, 1.0, 0, [[-1, E], [1, E]], 0)
            select(before[:], ALU.is_ge, 1.0, 0, [[-P, TB], [1, S]], -1)
            select(heads[:], ALU.is_ge, 0.0, 0, [[-HD, NH], [0, TOP]], 1)
            own(nc.gpsimd.memset(mean_row[:, TOP:SEL], 1.0 / S))
            own(nc.gpsimd.memset(top_row[:, TOP:SEL], 0.0))
            own.wait()
            select(heads[:], ALU.is_ge, 0.0, HD - 1, [[HD, NH], [0, TOP]], -1)
            own.wait()
            pool.sem_inc(pool_const, 1)

            def exact_root(g1):
                pool.wait_ge(dve_exvar, g1)
                nc.gpsimd.tensor_tensor(root0[:, 0:GT], var[:], half[:, 0:GT], ALU.pow).then_inc(pool_root, 1)

            def keep_xn(g1, tile):
                pool.wait_ge(dve_setup, 1)
                pool.wait_ge(dve_xn, g1)
                nc.gpsimd.tensor_copy(xn_all[:, bass.ds(tile, GT), :], xn[:]).then_inc(pool_xn, 1)

            def take(src, tile, s):
                nc.gpsimd.tensor_copy(grp[s][:], src[:, bass.ds(tile, GT), :]).then_inc(pool_grp, 1)

            def deviation(n2):
                pool.wait_ge(dve_var, n2)
                nc.gpsimd.tensor_tensor(sd[:], ve[:], half[:, 0:GT], ALU.pow).then_inc(pool_sd, 1)

            def place_w2(l, e):
                nc.gpsimd.tensor_copy(w2[:, e].rearrange("p c h -> p (c h)"),
                                      w2_raw[:, bass.ds(l * E + e, 1)].rearrange("p o c h -> p (o c h)")
                                      ).then_inc(pool_w2, 1)

            def place_bias(l):
                nc.gpsimd.tensor_copy(bias_l[:], bias1[:, bass.ds(l * (E * FC), E * FC)]).then_inc(pool_bias, 1)

            def store(c6, tile, s):
                pool.wait_ge(dve_y, c6)
                pool.sem_inc(pool_alone, 1)
                nc.gpsimd.tensor_copy(state[:, bass.ds(tile, GT), :], grp[s][:]).then_inc(pool_store, 1)

            exact_root(1)
            keep_xn(1, 0)
            exact_root(2)
            pool.wait_ge(pool_xn, 1)
            take(xn_all, 0, 0)
            deviation(1)
            keep_xn(2, GT)
            for l in range(1):
                pool.wait_ge(ld_w2[l], 16)
                for e in range(E):
                    place_w2(l, e)
            pool.wait_ge(dve_b1, 1)
            place_bias(0)
            pool.sem_inc(pool_store, 1)
            def step0(i, s, exact):
                n = i * 2 + s
                n1 = nc.gpsimd.snap(n + 1)
                n2 = nc.gpsimd.snap(n + 2)
                n3 = nc.gpsimd.snap(n + 3)
                c6 = nc.gpsimd.snap(n * E + (E + 2))
                tile = nc.gpsimd.snap(n * GT)
                pool.wait_ge(dve_setup, 1)
                pool.wait_ge(pool_store, n1)
                if exact or s == 0:
                    pool.wait_ge(pool_xn, n2)
                    take(xn_all, n * GT + GT, 1 - s)
                else:
                    take(state, 0, 1 - s)
                deviation(n2)
                if exact:
                    exact_root(n3)
                    keep_xn(n3, n * GT + 2 * GT)
                store(c6, tile, s)

            with pool.Fori(0, NG // 2 - 1) as i:
                for s in range(2):
                    step0(i, s, True)
            with pool.Fori(NG // 2 - 1, NG // 2) as i:
                for s in range(2):
                    step0(i, s, False)
            for l in range(1, L):
                pool.wait_ge(ld_w2[l], 16)
            with pool.Fori(1, L) as l:
                c = [nc.gpsimd.snap(l * (NG * E) + (e - E + 3)) for e in range(E)]
                pool.wait_ge(dve_setup, 1)
                pool.wait_ge(act_h[FC - 1], nc.gpsimd.snap(l * (NG * E) + 1))
                place_bias(l)
                for e in range(E):
                    pool.wait_ge(dve_setup, 1)
                    pool.wait_ge(pe_y, c[e])
                    place_w2(l, e)
                with pool.Fori(0, NG // 2) as i:
                    for s in range(2):
                        n = l * NG + i * 2 + s
                        n1 = nc.gpsimd.snap(n + 1)
                        n2 = nc.gpsimd.snap(n + 2)
                        c6 = nc.gpsimd.snap(n * E + (E + 2))
                        pool.wait_ge(dve_setup, 1)
                        pool.wait_ge(pool_store, n1)
                        take(state, nc.gpsimd.snap(((i * 2 + (s + 1)) % NG) * GT), 1 - s)
                        deviation(n2)
                        store(c6, nc.gpsimd.snap((i * 2 + s) * GT), s)

            pool.wait_ge(a_norm, 1)
            nc.gpsimd.tensor_tensor(root0[:], norm2[:], half[:], ALU.pow).then_inc(a_root, 1)
            pool.wait_ge(a_norm, 2)

            def bring(b, s):
                nc.gpsimd.tensor_copy(xb[s][:], xn_all[:, bass.ds(b * TB, TB), :])
                nc.gpsimd.tensor_copy(ecol[s][:], norm[:, bass.ds(b * TB, TB)])
                nc.gpsimd.tensor_copy(
                    eb[s][:], norm[:, bass.ds(b * TB, TB)].unsqueeze(2).to_broadcast([P, TB, P])).then_inc(a_in, 1)

            bring(0, 0)
            with pool.Fori(0, B // 2) as i:
                for s in range(2):
                    b1 = nc.gpsimd.snap(i * 2 + (s + 1))
                    pool.wait_ge(dve_setup, 1)
                    pool.wait_ge(a_res, b1)
                    bring(nc.gpsimd.snap((i * 2 + (s + 1)) % B), 1 - s)

        @block.vector
        def _(dve):
            V = nc.vector
            own = Own(dve, dve_seq)

            def wide(t, n, m=D):
                return t.unsqueeze(2).to_broadcast([P, n, m])

            def exact_variance(g1, tile):
                xg = x_in[:, bass.ds(tile, GT), :]
                k = own(V.tensor_reduce(lane[:], xg.rearrange("p t (k l) -> p t l k", l=16), X, ALU.add))
                own.wait(k)
                l4 = lane[:].rearrange("p t (a b c) -> p t a b c", a=2, b=2)
                k = own(V.tensor_tensor(lane8[:], l4[:, :, :, 0], l4[:, :, :, 1], ALU.add))
                own.wait(k)
                k = own(V.tensor_tensor(lane4[:], lane8[:, :, 0], lane8[:, :, 1], ALU.add))
                own.wait(k)
                l2 = lane4[:].rearrange("p t (a b) -> p t a b", b=2)
                k = own(V.tensor_tensor(lane2[:], l2[:, :, :, 0], l2[:, :, :, 1], ALU.add))
                own.wait(k)
                k = own(V.tensor_tensor(mean[:], lane2[:, :, 0], lane2[:, :, 1], ALU.add))
                own.wait(k)
                k = own(V.tensor_scalar(mean[:], mean[:], 1.0 / D, None, ALU.mult))
                own.wait(k)
                k = own(V.tensor_tensor(dev[:], xg, wide(mean[:], GT), ALU.subtract))
                own.wait(k)
                k = own(V.tensor_tensor(rem[:], dev[:], dev[:], ALU.mult))
                windows(rem, vsum[:], k)
                own(V.tensor_scalar(var[:], vsum[:], 1.0 / D, EPS, ALU.mult, ALU.add), dve_exvar)

            def windows(t, out, k):
                own.wait(k)
                k = own(V.tensor_reduce(win[:], t[:].rearrange("p t (w k) -> p t w k", w=4), X, ALU.add))
                own.wait(k)
                k = own(V.tensor_reduce(out, win[:], X, ALU.add))
                own.wait(k)

            def exact_sqrt(out, a, y, t):
                y_hi, y_lo, hh, hl, ll, r, iy = t
                k1 = own(V.tensor_single_scalar(y_hi.bitcast(u32), y.bitcast(u32), HIGH, ALU.bitwise_and))
                own(V.reciprocal(iy, y))
                own.wait(k1)
                k2 = own(V.tensor_tensor(y_lo, y, y_hi, ALU.subtract))
                k3 = own(V.tensor_tensor(hh, y_hi, y_hi, ALU.mult))
                own.wait(k2)
                own(V.tensor_tensor(hl, y_hi, y_lo, ALU.mult))
                own(V.tensor_tensor(ll, y_lo, y_lo, ALU.mult))
                own.wait(k3)
                own(V.tensor_tensor(r, a, hh, ALU.subtract))
                own.wait()
                own(V.scalar_tensor_tensor(hh, hl, -2.0, r, ALU.mult, ALU.add))
                own.wait()
                own(V.tensor_tensor(r, hh, ll, ALU.subtract))
                own.wait()
                own(V.scalar_tensor_tensor(hl, r, 0.5, iy, ALU.mult, ALU.mult))
                own.wait()
                return own(V.tensor_tensor(out, y, hl, ALU.add))

            def exact_quotient(g1, g0, tile):
                dve.wait_ge(pool_root, g1)
                k = exact_sqrt(sd_x[:], var[:], root0[:, 0:GT], [t[:, 0:GT] for t in sqs[0:7]])
                own.wait(k)
                k1 = own(V.tensor_single_scalar(sd_hi[:].bitcast(u32), sd_x[:].bitcast(u32), HIGH, ALU.bitwise_and))
                k2 = own(V.reciprocal(inv[:], sd_x[:]))
                own.wait(k1)
                own(V.tensor_tensor(sd_lo[:], sd_x[:], sd_hi[:], ALU.subtract))
                own.wait(k2)
                own(V.tensor_scalar(ninv[:], inv[:], -1.0, None, ALU.mult))
                k = own(V.tensor_tensor(q0[:], dev[:], wide(inv[:], GT), ALU.mult))
                own.wait(k)
                k = own(V.tensor_single_scalar(q_hi[:].bitcast(u32), q0[:].bitcast(u32), HIGH, ALU.bitwise_and))
                own.wait(k)
                k = own(V.tensor_tensor(q_lo[:], q0[:], q_hi[:], ALU.subtract))
                last = [k] * GT
                for q, sd_part, other in ((q_hi, sd_hi, dev), (q_hi, sd_lo, rem), (q_lo, sd_hi, rem),
                                          (q_lo, sd_lo, rem)):
                    for t in range(GT):
                        own.wait(last[t])
                        last[t] = own(V.scalar_tensor_tensor(
                            rem[:, t], q[:, t], sd_part[:, t:t + 1], other[:, t], ALU.mult,
                            ALU.subtract if other is dev else ALU.add))
                if g0 is not None:
                    dve.wait_ge(pool_xn, g0)
                for t in range(GT):
                    own.wait(last[t])
                    ins = V.scalar_tensor_tensor(xn[:, t], rem[:, t], ninv[:, t:t + 1], q0[:, t],
                                                 ALU.mult, ALU.add)
                    own(ins, dve_xn) if t == GT - 1 else own(ins)
                dve.wait_ge(dve_xn, g1)
                k = own(V.tensor_tensor(rem[:], xn[:], xn[:], ALU.mult))
                windows(rem, norm2[:, bass.ds(tile, GT)], k)

            def place_w1(l, e):
                w1_g = w1_gs[e % 2]
                own(V.tensor_scalar(w1_g[:], w1_raw[:, bass.ds(l * E + e, 1)].rearrange("p o f -> p (o f)"),
                                    cols[:, bass.ds(l * E + (COL_G + e), 1)], None, ALU.mult))
                own.wait()
                own(V.tensor_copy(w1_hi[:, e], w1_g[:]))
                own.wait()
                own(V.tensor_tensor(w1_lo[:, e], w1_g[:], w1_hi[:, e].bitcast(fp32), ALU.subtract), dve_w1)

            def group_stats(s, n2):
                dve.wait_ge(pool_grp, n2)
                for t in range(GT):
                    own(V.bn_stats(stats[:, t], grp[s][:, t]))
                own.wait()
                for t in range(GT):
                    own(V.bn_aggr(mv[:, t], stats[:, t]))
                own.wait()
                own(V.tensor_scalar(ve[:], mv[:, :, 1], EPS, None, ALU.add), dve_var)

            def normalise(s, n1, n2):
                dve.wait_ge(pool_sd, n2)
                own(V.reciprocal(rsd[:], sd[:]))
                own.wait()
                if n1 is not None:
                    dve.wait_ge(pe_xT, n1)
                for t in range(GT):
                    ins = V.tensor_scalar(xhat[:, t], grp[s][:, t], mv[:, t, 0:1], rsd[:, t:t + 1],
                                          ALU.subtract, ALU.mult)
                    own(ins, dve_xhat) if t == GT - 1 else own(ins)

            def split_xT(s, n2):
                dve.wait_ge(pe_xT, n2)
                own(V.tensor_copy(xT_hi[s][:], t_ps[:]))
                own.wait()
                own(V.tensor_tensor(xT_lo[s][:], t_ps[:], xT_hi[s][:].bitcast(fp32), ALU.subtract), dve_xT)

            def rank_experts(s, n2, col):
                def over(t):
                    return t[:, bass.ds(col, E)].unsqueeze(1).to_broadcast([P, GT, E])

                own(V.tensor_tensor(lg_a[:], over(rw_sum), wide(mv[:, :, 0], GT, E), ALU.mult))
                own.wait()
                own(V.tensor_tensor(lg_a[:], lg_a[:], over(rb), ALU.add))
                dve.wait_ge(pe_lg, n2)
                own(V.tensor_tensor(lg[:], m_ps[:, 0:GT * E].rearrange("p (t e) -> p t e", e=E),
                                    wide(sd[:], GT, E), ALU.mult))
                own.wait()
                own(V.tensor_tensor(lg[:], lg[:], lg_a[:], ALU.add))
                own.wait()
                mine = lg[:].unsqueeze(3).to_broadcast([P, GT, E, E])
                other = lg[:].unsqueeze(2).to_broadcast([P, GT, E, E])
                own(V.tensor_tensor(cmp_eq[:], other, mine, ALU.is_equal))
                own(V.tensor_tensor(cmp_gt[:], other, mine, ALU.is_gt))
                own.wait(own.n - 1)
                own(V.tensor_tensor(cmp_eq[:], cmp_eq[:],
                                    before4[:].unsqueeze(1).to_broadcast([P, GT, E, E]), ALU.mult))
                own.wait()
                own(V.tensor_tensor(cmp_gt[:], cmp_gt[:], cmp_eq[:], ALU.add))
                own.wait()
                own(V.tensor_reduce(place[:], cmp_gt[:], X, ALU.add))
                own.wait()
                own(V.tensor_scalar(chosen[:], place[:], K_TOP - 0.5, None, ALU.is_lt))
                own.wait()
                own(V.tensor_tensor(lg_a[:], lg[:], chosen[:], ALU.mult))
                own.wait()
                own(V.tensor_reduce(two[:], lg_a[:], X, ALU.add))
                own.wait()
                own(V.scalar_tensor_tensor(arg[:], wide(two[:], GT, E), -0.5, lg[:], ALU.mult, ALU.add), dve_arg)

            def combine(s, n2):
                dve.wait_ge(act_th, n2)
                own(V.tensor_scalar(th[:], th[:], 0.5, 0.5, ALU.mult, ALU.add))
                own.wait()
                own(V.tensor_tensor(comb[s][:], th[:], chosen[:], ALU.mult), dve_comb)

            def keep_combT(n2):
                dve.wait_ge(pe_combT, n2)
                own(V.tensor_copy(combT[:], m_ps[0:E, :]), dve_combT)

            def add_z(s, n1):
                dve.wait_ge(pe_z, n1)
                own(V.tensor_tensor(grp[s][:], m_ps[:].rearrange("p (t h) -> p t h", h=D), grp[s][:],
                                    ALU.add), dve_z)
                own.wait()

            def add_y(s, e, c3):
                dve.wait_ge(pe_y, c3)
                own.wait()
                for t in range(GT):
                    ins = V.scalar_tensor_tensor(grp[s][:, t], y_ps[e % 2][:, t * D:(t + 1) * D],
                                                 comb[s][:, t, e:e + 1], grp[s][:, t], ALU.mult, ALU.add)
                    own(ins, dve_y) if t == GT - 1 else own(ins)

            dve.wait_ge(ld_x[0], 16)
            exact_variance(1, 0)
            dve.wait_ge(pe_setup, 1)
            own(V.tensor_copy(cols[:], t_ps[:, 0:NCOL]))
            dve.wait_ge(pe_setup, 2)
            own(V.tensor_copy(projT[:].rearrange("p c h -> p (c h)"), m_ps[:]))
            dve.wait_ge(pe_setup, 3)
            own(V.tensor_copy(rw_sum[:], y_ps[0][:, 0:LE1]))
            own(V.tensor_copy(rw_hi[:], rw[:]))
            own.wait()
            own(V.tensor_tensor(rw_lo[:], rw[:], rw_hi[:].bitcast(fp32), ALU.subtract), dve_setup)
            exact_quotient(1, None, 0)
            dve.wait_ge(ld_x[1], 16)
            own.wait()
            exact_variance(2, GT)
            group_stats(0, 1)
            normalise(0, None, 1)
            split_xT(0, 1)
            rank_experts(0, 1, 0)
            combine(0, 1)
            keep_combT(1)
            exact_quotient(2, 1, GT)
            dve.wait_ge(ld_w1, 16 * L)
            for e in range(E):
                place_w1(0, e)
            dve.wait_ge(pe_b1, 1)
            own(V.tensor_tensor(bias1[:], y_ps[1][:, 0:NB1], cols[:, COL_B1:COL_QKV], ALU.add), dve_b1)
            for g in range(2, NG):
                dve.wait_ge(ld_x[g], 16)
            dve.sem_inc(dve_y, 2)

            def step(l, i, s, exact=False):
                n = l * NG + i * 2 + s
                c = {k: V.snap(n * E + k) for k in range(3, E + 3)}
                n1, n2 = V.snap(n + 1), V.snap(n + 2)
                add_z(s, n1)
                group_stats(1 - s, n2)
                add_y(s, 0, c[3])
                normalise(1 - s, n1, n2)
                if exact:
                    n3 = V.snap(n + 3)
                    tile = V.snap(n * GT + 2 * GT)
                    exact_variance(n3, tile)
                add_y(s, 1, c[4])
                split_xT(1 - s, n2)
                if exact:
                    exact_quotient(n3, n2, tile)
                add_y(s, 2, c[5])
                rank_experts(1 - s, n2, V.snap(((n + 1) // NG) * E))
                combine(1 - s, n2)
                add_y(s, 3, c[6])
                keep_combT(n2)
                own.clear()

            own.clear()
            with dve.Fori(0, NG // 2 - 1) as i:
                for s in range(2):
                    step(0, i, s, exact=True)
            with dve.Fori(NG // 2 - 1, NG // 2) as i:
                for s in range(2):
                    step(0, i, s)
            with dve.Fori(1, L) as l:
                for e in range(E):
                    place_w1(l, e)
                own.clear()
                with dve.Fori(0, NG // 2) as i:
                    for s in range(2):
                        step(l, i, s)

            own(V.memset(ctxT[:], 0.0), a_norm)
            dve.wait_ge(a_root, 1)
            exact_sqrt(norm[:], norm2[:], root0[:], [t[:] for t in sqs[0:7]])
            own.wait()
            own(V.memset(mx[:], 0.0), a_norm)

            def rank_tokens(b1, s):
                dve.wait_ge(a_rowE, b1)
                for a in range(TB):
                    e_a = ecol[s][:, a:a + 1]
                    own(V.tensor_scalar(gt_out[:], bank[0][:, 0:S], e_a, None, ALU.is_gt, ALU.add,
                                        accum_out=n_gt[:, a:a + 1]))
                    own(V.scalar_tensor_tensor(eq_out[:], bank[0][:, 0:S], e_a, before[:, a], ALU.is_equal,
                                               ALU.mult, accum_out=n_eq[:, a:a + 1]))
                    own.wait()
                own(V.tensor_tensor(rank[:], n_gt[:], n_eq[:], ALU.add))
                own.wait()
                own(V.tensor_scalar(rank[:], rank[:], float(TOP), None, ALU.min))
                own.wait()
                own(V.tensor_tensor(onehot[:], slot[:].unsqueeze(1).to_broadcast([P, TB, SEL]),
                                    wide(rank[:], TB, SEL), ALU.is_equal), a_oh)

            def keep_xq(b1, s):
                dve.wait_ge(a_xq, b1)
                own(V.tensor_copy(xqT[:], bank[2][:, 0:SEL]), a_xqs)
                own(V.tensor_copy(onehotT[s][0:SEL, :], bank[2][0:SEL, P:P + S]), a_ohTs)

            def spread_q(b1, s):
                dve.wait_ge(a_q, b1)
                own(V.tensor_scalar(qT[:, 0:TOP], bank[2][:, 0:TOP], cols[:, COL_QKV:COL_QKV + 1], None, ALU.add))
                own.wait()
                own(V.tensor_tensor(qbd[s][:], qT[:, 0:TOP].unsqueeze(1).to_broadcast([P, NH, TOP]),
                                    heads[:], ALU.mult), a_qbd)

            rank_tokens(1, 0)
            keep_xq(1, 0)
            spread_q(1, 0)
            own.clear()
            with dve.Fori(0, B // 2) as i:
                for s in range(2):
                    b1, b2_ = V.snap(i * 2 + (s + 1)), V.snap(i * 2 + (s + 2))
                    dve.wait_ge(a_sc, b1)
                    for c in range(CH // 2):
                        own(V.tensor_reduce(mx[0:QC, 2 * c:2 * c + 2],
                                            bank[4 + c][0:QC, :].rearrange("p (c s) -> p c s", s=S), X, ALU.max))
                    own.wait()
                    own(V.tensor_scalar(nmx[0:QC, :], mx[0:QC, :], -SCALE, None, ALU.mult), a_mx)
                    rank_tokens(b2_, 1 - s)
                    dve.wait_ge(a_exp, b1)
                    own(V.reciprocal(rden[0:QC, :], den[0:QC, :]))
                    own.wait()
                    for c in range(CH):
                        ins = V.tensor_scalar(prob[0:QC, c], prob[0:QC, c], rden[0:QC, c:c + 1], None, ALU.mult)
                        own(ins, a_pr) if c == CH - 1 else own(ins)
                    keep_xq(b2_, 1 - s)
                    dve.wait_ge(a_pt, b1)
                    own(V.tensor_copy(pT[:, 0, :], bank[6][:, 0:NH * TOP]), a_pt0)
                    spread_q(b2_, 1 - s)
                    dve.wait_ge(a_cx, b1)
                    own(V.tensor_tensor(picked[:], bank[4][:, 0:NH * TOP].rearrange("p (h q) -> p h q", q=TOP),
                                        heads[:], ALU.mult))
                    own.wait()
                    own(V.tensor_reduce(cx[:], picked[:].rearrange("p h q -> p q h"), X, ALU.add))
                    own.wait()
                    own(V.tensor_scalar(ctxT[:, 0:TOP], cx[:], cols[:, COL_QKV + 2:COL_QKV + 3], None,
                                        ALU.add), a_cxs)
                    tiles = V.snap(i * (2 * TB) + s * TB)
                    dve.wait_ge(st_out[s], V.snap(i * 16 + 16))
                    dve.wait_ge(a_out, b1)
                    own(V.tensor_tensor(sum1[:], bank[6][:, 0:TB * D].rearrange("p (t h) -> p t h", h=D),
                                        state[:, bass.ds(tiles, TB), :], ALU.add))
                    own.wait()
                    own(V.tensor_tensor(out_sb[s][:], sum1[:], x_in[:, bass.ds(tiles, TB), :], ALU.add), a_outs)
                    own.clear()

        @block.tensor
        def _(pe):
            T = nc.tensor
            pe.wait_ge(pool_const, 1)
            pe.wait_ge(ld_rows, 64)
            T.transpose(t_ps[:, 0:NCOL], rows[0:NCOL, :], ident[0:NCOL, 0:NCOL]).then_inc(pe_setup, 1)
            pe.wait_ge(ld_proj, 32)
            for c in range(4):
                ins = T.transpose(m_ps[:, c * D:(c + 1) * D], proj[:, c, :], ident[:])
            ins.then_inc(pe_setup, 1)
            pe.wait_ge(ld_small, 64)
            T.matmul(y_ps[0][:, 0:LE1], ones[:], rw[:], start=True, stop=True).then_inc(pe_setup, 1)
            pe.wait_ge(dve_setup, 1)

            def transpose_x(n2, n1):
                pe.wait_ge(dve_xhat, n2)
                if n1 is not None:
                    pe.wait_ge(dve_xT, n1)
                for t in range(GT):
                    ins = T.transpose(t_ps[:, t * P:(t + 1) * P], xhat[:, t], ident[:])
                ins.then_inc(pe_xT, 1)

            def route(s, n2, n1, col):
                pe.wait_ge(dve_xT, n2)
                if n1 is not None:
                    pe.wait_ge(dve_z, n1)
                for t in range(GT):
                    o = m_ps[:, t * E:(t + 1) * E]
                    hi, lo = (x[s][:, t * P:(t + 1) * P] for x in (xT_hi, xT_lo))
                    T.matmul(o, hi, rw_hi[:, bass.ds(col, E)], start=True, stop=False)
                    T.matmul(o, hi, rw_lo[:, bass.ds(col, E)], start=False, stop=False)
                    ins = T.matmul(o, lo, rw_hi[:, bass.ds(col, E)], start=False, stop=True)
                ins.then_inc(pe_lg, 1)

            def transpose_comb(s, n2):
                pe.wait_ge(dve_comb, n2)
                for t in range(GT):
                    ins = T.transpose(m_ps[0:E, t * P:(t + 1) * P], comb[s][:, t], ident[:])
                ins.then_inc(pe_combT, 1)

            def second_bias(n1, l):
                pe.wait_ge(pool_const, 1)
                pe.wait_ge(dve_combT, n1)
                for t in range(GT):
                    ins = T.matmul(m_ps[:, t * D:(t + 1) * D], combT[:, t * P:(t + 1) * P],
                                   b2[:, bass.ds(l, 1), :].rearrange("e o h -> e (o h)"), start=True, stop=True)
                ins.then_inc(pe_z, 1)

            def hidden(s, e, c, w):
                pe.wait_ge(dve_w1, w)
                for f in range(FC):
                    pe.wait_ge(act_h[f], c)
                    hi, lo = (x[:, e, f * P:(f + 1) * P] for x in (w1_hi, w1_lo))
                    T.matmul(h_ps[f][:], hi, xT_hi[s][:], start=True, stop=False)
                    T.matmul(h_ps[f][:], hi, xT_lo[s][:], start=False, stop=False)
                    T.matmul(h_ps[f][:], lo, xT_hi[s][:], start=False, stop=True).then_inc(pe_h[f], 1)

            def outputs(e, c1, c2, w):
                pe.wait_ge(dve_y, c1)
                pe.wait_ge(pool_w2, w)
                for t in range(GT):
                    for f in range(FC):
                        if t == 0:
                            pe.wait_ge(act_h[f], c2)
                        ins = T.matmul(y_ps[e % 2][:, t * D:(t + 1) * D], hid[e % 2][:, f, t * P:(t + 1) * P],
                                       w2[:, e, f], start=(f == 0), stop=(f == FC - 1))
                ins.then_inc(pe_y, 1)

            transpose_x(1, None)
            route(0, 1, None, 0)
            transpose_comb(0, 1)
            pe.wait_ge(ld_w1, 16 * L)
            for m in range(L * E):
                for f in range(FC):
                    ins = T.matmul(y_ps[1][:, m * FC + f:m * FC + f + 1], w1_raw[:, m, f * P:(f + 1) * P],
                                   cols[:, COL_B + m:COL_B + m + 1], start=True, stop=True)
            ins.then_inc(pe_b1, 1)
            pe.wait_ge(dve_b1, 1)
            pe.sem_inc(pe_y, 2)
            with pe.Fori(0, L) as l:
                w = [T.snap(l * E + (e + 1)) for e in range(E)]
                with pe.Fori(0, NG // 2) as i:
                    for s in range(2):
                        n = l * NG + i * 2 + s
                        c = {k: T.snap(n * E + k) for k in range(1, E + 2)}
                        n1, n2 = T.snap(n + 1), T.snap(n + 2)
                        hidden(s, 0, c[1], w[0])
                        second_bias(n1, l)
                        hidden(s, 1, c[2], w[1])
                        outputs(0, c[1], c[2], w[0])
                        hidden(s, 2, c[3], w[2])
                        outputs(1, c[2], c[3], w[1])
                        transpose_x(n2, n1)
                        hidden(s, 3, c[4], w[3])
                        outputs(2, c[3], c[4], w[2])
                        route(1 - s, n2, n1, T.snap(((n + 1) // NG) * E))
                        outputs(3, c[4], c[5], w[3])
                        transpose_comb(1 - s, n2)

            def row_first(b1, s):
                pe.wait_ge(a_in, b1)
                for a in range(TB):
                    ins = T.transpose(bank[0][:, a * P:(a + 1) * P], eb[s][:, a], ident[:])
                ins.then_inc(a_rowE, 1)
                for a in range(TB):
                    ins = T.transpose(bank[1][:, a * P:(a + 1) * P], xb[s][:, a], ident[:])
                ins.then_inc(a_xbT, 1)

            def row_kv(b1):
                pe.wait_ge(a_xbTs, b1)
                T.matmul(bank[3][:, 0:S], projT[:, 1], xbT[:], start=True, stop=True)
                for a in range(TB):
                    ins = T.matmul(bank[3][:, S + a * D:S + (a + 1) * D], xbT[:, a * P:(a + 1) * P],
                                   projT[:, 2], start=True, stop=True)
                ins.then_inc(a_kv, 1)

            def row_select(b1, s):
                pe.wait_ge(a_oh, b1)
                for a in range(TB):
                    T.transpose(bank[2][0:SEL, (1 + a) * P:(2 + a) * P], onehot[:, a], ident[:])
                for a in range(TB):
                    ins = T.matmul(bank[2][:, 0:SEL], xb[s][:, a], onehot[:, a], start=(a == 0), stop=(a == TB - 1))
                ins.then_inc(a_xq, 1)

            def row_q(b1):
                pe.wait_ge(a_xqs, b1)
                pe.wait_ge(a_ohTs, b1)
                T.matmul(bank[2][:, 0:SEL], projT[:, 0], xqT[:], start=True, stop=True).then_inc(a_q, 1)

            row_first(1, 0)
            row_kv(1)
            row_select(1, 0)
            row_q(1)
            pe.sem_inc(a_res, 1)
            with pe.Fori(0, B // 2) as i:
                for s in range(2):
                    b1, b2_ = T.snap(i * 2 + (s + 1)), T.snap(i * 2 + (s + 2))
                    pe.wait_ge(a_qbd, b1)
                    pe.wait_ge(a_vs, b1)
                    for c in range(CH):
                        ins = T.matmul(
                            bank[4 + c // 2][0:QC, (c % 2) * S:(c % 2 + 1) * S],
                            qbd[s][:].rearrange("p h q -> p (h q)")[:, c * QC:(c + 1) * QC], kT[s][:],
                            start=True, stop=True)
                    ins.then_inc(a_sc, 1)
                    row_first(b2_, 1 - s)
                    row_kv(b2_)
                    row_select(b2_, 1 - s)
                    pe.wait_ge(a_pr, b1)
                    for a in range(TB):
                        for c in range(CH):
                            ins = T.transpose(bank[6 + a][:, c * QC:(c + 1) * QC],
                                              prob[0:QC, c, a * P:(a + 1) * P], ident[0:QC, 0:QC])
                    ins.then_inc(a_pt, 1)
                    row_q(b2_)
                    pe.wait_ge(a_pt0, b1)
                    T.matmul(bank[4][:, 0:NH * TOP], v[s][:, 0], pT[:, 0], start=True, stop=False)
                    pe.wait_ge(a_pt1, b1)
                    T.matmul(bank[4][:, 0:NH * TOP], v[s][:, 1], pT[:, 1], start=False, stop=True).then_inc(a_cx, 1)
                    for a in range(TB):
                        T.matmul(bank[5][0:SEL, 0:D], mean_row[:], xb[s][:, a], start=(a == 0), stop=False)
                    T.matmul(bank[5][0:SEL, 0:D], top_row[:], ob[:], start=False, stop=False)
                    pe.wait_ge(a_cxs, b1)
                    T.matmul(bank[5][0:SEL, 0:D], ctxT[:], projT[:, 3], start=False, stop=True).then_inc(a_res, 1)
                    pe.wait_ge(a_ress, b1)
                    for a in range(TB):
                        ins = T.matmul(bank[6][:, a * D:(a + 1) * D], onehotT[s][0:SEL, a * P:(a + 1) * P],
                                       res[0:SEL, :], start=True, stop=True)
                    ins.then_inc(a_out, 1)


_INS = ["L0_attn_x", "L0_attn_in_proj_w", "L0_attn_in_proj_b", "L0_attn_out_w", "L0_attn_out_b",
        "L0_ffn_router_w", "L0_ffn_router_b", "L0_ffn_ln_g", "L0_ffn_ln_b", "L0_ffn_w1", "L0_ffn_b1",
        "L0_ffn_w2", "L0_ffn_b2"]


def kernel(**inputs):
    import numpy as _np
    import concourse.bacc as _bacc
    from concourse import mybir as _mybir
    from concourse.bass_utils import run_bass_kernel_spmd as _run

    nc = _bacc.Bacc("TRN2", target_bir_lowering=False, num_devices=1)
    arrays, args = {}, []
    for name in _INS:
        a = _np.ascontiguousarray(inputs[name])
        arrays[f"in_{name}"] = a
        args.append(nc.dram_tensor(f"in_{name}", a.shape, _mybir.dt.from_np(a.dtype), kind="ExternalInput").ap())
    shape = inputs["L0_attn_x"].shape
    args.append(nc.dram_tensor("out", shape, _mybir.dt.float32, kind="ExternalOutput").ap())
    attention_and_experts_kernel(nc, *args)
    r = _run(nc, [arrays], core_ids=[0])
    return r.results[0]["out"]
```

```python
import concourse.bass as bass
from concourse import mybir
from contextlib import ExitStack


def attention_and_experts_kernel(
    nc: bass.Bass,
    x_dram: bass.AP,
    in_proj_w: bass.AP,
    in_proj_b: bass.AP,
    out_w: bass.AP,
    out_b: bass.AP,
    router_w: bass.AP,
    router_b: bass.AP,
    ln_g: bass.AP,
    ln_b: bass.AP,
    w1_dram: bass.AP,
    b1_dram: bass.AP,
    w2_dram: bass.AP,
    b2_dram: bass.AP,
    out_dram: bass.AP,
):
    fp32 = mybir.dt.float32
    fp32r = mybir.dt.float32r
    u32 = mybir.dt.uint32
    ALU = mybir.AluOpType
    ACT = mybir.ActivationFunctionType
    X = mybir.AxisListType.X

    B, S, D = x_dram.shape
    P = 128
    TB = S // P
    NT = B * TB
    L, E, _, F = w1_dram.shape
    FC = F // P
    GT = 4
    NG = NT // GT
    GN = GT * P
    EPS = 1e-5
    NH = 16
    HD = D // NH
    TOP = 27
    SEL = TOP + 1
    CH = 4
    HC = NH // CH
    QC = HC * TOP
    SCALE = float(HD) ** -0.5
    HIGH = 0xFFFFF000
    K_TOP = 2
    LX = 2
    NX = LX * NG

    x_v = x_dram.rearrange("b (t p) h -> p (b t) h", p=P)
    out_v = out_dram.rearrange("b (t p) h -> p (b t) h", p=P)

    ctx = ExitStack()
    with ctx:
        def sb(name, shape, dt=fp32):
            return ctx.enter_context(nc.sbuf_tensor(name, shape, dt))

        def sem(name):
            return ctx.enter_context(nc.semaphore(name))

        x_in = sb("x_in", [P, NT, D])
        xn_all = sb("xn_all", [P, NT, D])
        state = sb("state", [P, NT, D])
        raw = sb("raw", [P, L * E * 2 * F])
        raw_v = raw[:].rearrange("p (l w e f) -> p l w e f", w=2, e=E, f=F)
        w1_raw = raw_v[:, :, 0]
        w2_raw = raw_v[:, :, 1]
        w1_hi = sb("w1_hi", [P, E, F], fp32r)
        w1_lo = sb("w1_lo", [P, E, F], fp32r)
        w1_gs = [sb(f"w1_g{i}", [P, F]) for i in range(2)]
        w2 = sb("w2", [P, E, FC, D])
        NB1 = L * E * FC
        COL_G, COL_B, COL_B1, COL_QKV = 0, L * E, 2 * L * E, 2 * L * E + NB1
        NCOL = COL_QKV + 3
        rows = sb("rows", [P, P])
        cols = sb("cols", [P, NCOL])
        bias1 = sb("bias1", [P, NB1])
        bias_l = sb("bias_l", [P, E * FC])
        LE1 = (L + 1) * E
        rw = sb("rw", [P, LE1])
        rw_hi = sb("rw_hi", [P, LE1], fp32r)
        rw_lo = sb("rw_lo", [P, LE1], fp32r)
        rb = sb("rb", [P, LE1])
        rw_sum = sb("rw_sum", [P, LE1])
        b2 = sb("b2", [E, L + 1, D])
        proj = sb("proj", [P, 4, D])
        projT = sb("projT", [P, 4, D])
        ob = sb("ob", [1, D])
        ident = sb("ident", [P, P])
        ones = sb("ones", [P, P])
        before4 = sb("before4", [P, E, E])
        before = sb("before", [P, TB, S])
        slot = sb("slot", [P, SEL])
        heads = sb("heads", [P, NH, TOP])
        mean_col = sb("mean_col", [P, 1])
        top_row = sb("top_row", [1, SEL])
        half = sb("half", [P, NT])
        grp = [sb(f"grp{i}", [P, GT, D]) for i in range(2)]
        xhat = sb("xhat", [P, GT, D])
        xT_hi = [sb(f"xT_hi{i}", [P, GN], fp32r) for i in range(2)]
        xT_lo = [sb(f"xT_lo{i}", [P, GN], fp32r) for i in range(2)]
        hid = [sb(f"hid{i}", [P, FC, GN]) for i in range(2)]
        stats = sb("stats", [P, GT, 6])
        mv = sb("mv", [P, GT, 2])
        ve = sb("ve", [P, GT])
        sd = sb("sd", [P, GT])
        rsd = sb("rsd", [P, GT])
        lg = sb("lg", [P, GT, E])
        lg_a = sb("lg_a", [P, GT, E])
        arg = sb("arg", [P, GT, E])
        th = sb("th", [P, GT, E])
        cmp_gt = sb("cmp_gt", [P, GT, E, E])
        cmp_eq = sb("cmp_eq", [P, GT, E, E])
        place = sb("place", [P, GT, E])
        chosen = sb("chosen", [P, GT, E])
        two = sb("two", [P, GT])
        comb = [sb(f"comb{i}", [P, GT, E]) for i in range(2)]
        combT = sb("combT", [E, GN])
        stats0 = sb("stats0", [P, GT, 6])
        mv0 = sb("mv0", [P, NT, 2])
        ve0 = sb("ve0", [P, NT])
        sd0 = sb("sd0", [P, NT])
        rsd0 = sb("rsd0", [P, NT])
        nmean0 = sb("nmean0", [P, NT])
        lane = sb("lane", [P, GT, 16])
        lane8 = sb("lane8", [P, GT, 2, 4])
        lane4 = sb("lane4", [P, GT, 4])
        lane2 = sb("lane2", [P, GT, 2])
        mean = sb("mean", [P, GT])
        dev = sb("dev", [P, GT, D])
        q0 = sb("q0", [P, GT, D])
        q_hi = sb("q_hi", [P, GT, D])
        q_lo = sb("q_lo", [P, GT, D])
        rem = sb("rem", [P, GT, D])
        xn = sb("xn", [P, GT, D])
        win = sb("win", [P, GT, 4])
        vsum = sb("vsum", [P, GT])
        var = sb("var", [P, GT])
        sqs = [sb(f"sqs{i}", [P, GT]) for i in range(7)]
        norm2 = sb("norm2", [P, GT])
        norm = sb("norm", [P, NT])
        sd_x = sb("sd_x", [P, GT])
        sd_hi = sb("sd_hi", [P, GT])
        sd_lo = sb("sd_lo", [P, GT])
        inv = sb("inv", [P, GT])
        ninv = sb("ninv", [P, GT])
        root0 = sb("root0", [P, GT])
        at = [0]

        def carve(n):
            at[0] += n
            return raw[:, at[0] - n:at[0]]

        xb = [carve(TB * D).rearrange("p (t h) -> p t h", h=D) for _ in range(2)]
        eb = [carve(TB * P).rearrange("p (t h) -> p t h", h=P) for _ in range(2)]
        ecol = [carve(TB) for _ in range(2)]
        xbT = carve(S)
        kT = [carve(S) for _ in range(2)]
        v = [carve(TB * D).rearrange("p (t h) -> p t h", h=D) for _ in range(2)]
        gt_out = carve(S)
        eq_out = carve(S)
        n_gt = carve(TB)
        n_eq = carve(TB)
        rank = carve(TB)
        onehot = carve(TB * SEL).rearrange("p (t q) -> p t q", q=SEL)
        onehotT = [carve(S) for _ in range(2)]
        xqT = carve(SEL)
        qT = carve(SEL)
        qbd = [carve(NH * TOP).rearrange("p (h q) -> p h q", q=TOP) for _ in range(2)]
        prob = carve(CH * S).rearrange("p (c s) -> p c s", s=S)
        mx = carve(CH)
        nmx = carve(CH)
        den = carve(CH)
        rden = carve(CH)
        pT = carve(TB * NH * TOP).rearrange("p (t r) -> p t r", t=TB)
        picked = carve(NH * TOP).rearrange("p (h q) -> p h q", q=TOP)
        cx = carve(TOP)
        ctxT = carve(SEL)
        res = carve(D)
        meanT = [carve(SEL) for _ in range(2)]
        bank = [ctx.enter_context(nc.psum_tensor(f"bank{i}", [P, GN], fp32)) for i in range(8)]
        h_ps = [bank[0], bank[1], bank[2], bank[0]]
        y_ps = bank[3:5]
        a_ps, t_ps, m_ps = bank[5], bank[6], bank[7]

        ld_x = [sem(f"ld_x{g}") for g in range(NG)]
        ld_rows = sem("ld_rows")
        ld_w1, ld_w2 = ([sem(f"ld_w{w}_{l}") for l in range(L)] for w in (1, 2))
        ld_proj, ld_small = sem("ld_proj"), sem("ld_small")
        pool_seq = sem("pool_seq")
        pool_const = sem("pool_const")
        pool_w2 = sem("pool_w2")
        pool_bias = sem("pool_bias")
        pool_alone = sem("pool_alone")
        pool_sd0 = sem("pool_sd0")
        pool_grp = sem("pool_grp")
        pool_sd = sem("pool_sd")
        pool_root = sem("pool_root")
        pool_xn = sem("pool_xn")
        pool_store = sem("pool_store")
        dve_seq = sem("dve_seq")
        dve_setup = sem("dve_setup")
        dve_var0 = sem("dve_var0")
        dve_rsd0 = sem("dve_rsd0")
        dve_b1 = sem("dve_b1")
        dve_w1 = sem("dve_w1")
        dve_var = sem("dve_var")
        dve_xhat = sem("dve_xhat")
        dve_xT = sem("dve_xT")
        dve_arg = sem("dve_arg")
        dve_comb = sem("dve_comb")
        dve_combT = sem("dve_combT")
        dve_z = sem("dve_z")
        dve_y = sem("dve_y")
        dve_square = sem("dve_square")
        dve_xn = sem("dve_xn")
        pe_setup = sem("pe_setup")
        pe_b1 = sem("pe_b1")
        pe_xT = sem("pe_xT")
        pe_lg = sem("pe_lg")
        pe_combT = sem("pe_combT")
        pe_z = sem("pe_z")
        pe_h = [sem(f"pe_h{f}") for f in range(FC)]
        pe_y = sem("pe_y")
        act_h = [sem(f"act_h{f}") for f in range(FC)]
        act_th = sem("act_th")
        act_seq = sem("act_seq")
        act_xn0 = sem("act_xn0")
        pool_row = sem("pool_row")
        pe_row = sem("pe_row")
        act_xbT = sem("act_xbT")
        pe_kv = sem("pe_kv")
        act_kv = sem("act_kv")
        dve_onehot = sem("dve_onehot")
        pe_xq = sem("pe_xq")
        dve_xq = sem("dve_xq")
        pe_q = sem("pe_q")
        dve_qbd = sem("dve_qbd")
        pe_sc = sem("pe_sc")
        dve_mx = sem("dve_mx")
        act_exp = sem("act_exp")
        dve_prob = sem("dve_prob")
        pe_pT = sem("pe_pT")
        dve_pT = sem("dve_pT")
        act_pT = sem("act_pT")
        pe_cx = sem("pe_cx")
        dve_cx = sem("dve_cx")
        pe_res = sem("pe_res")
        act_res = sem("act_res")
        pe_out = sem("pe_out")
        dve_out = sem("dve_out")
        dve_final = sem("dve_final")
        st_out = sem("st_out")

        class Own:

            def __init__(self, eng, s):
                self.eng, self.s, self.n = eng, s, 0

            def __call__(self, ins, instead=None):
                if instead is not None:
                    ins.then_inc(instead, 1)
                else:
                    self.n += 1
                    ins.then_inc(self.s, 1)
                return self.n

            def wait(self, n=None):
                n = self.n if n is None else n
                if n > 0:
                    self.eng.wait_ge(self.s, n)

            def clear(self):
                self.wait()
                self.eng.sem_clear(self.s)
                self.n = 0

        block = ctx.enter_context(nc.Block())

        @block.sync
        def _(sp):
            def load_x(g):
                sp.dma_start(x_in[:, g * GT:(g + 1) * GT, :],
                             x_v[:, g * GT:(g + 1) * GT, :]).then_inc(ld_x[g], 16)

            load_x(0)
            sp.dma_start(rows[COL_G:COL_B, :], ln_g.rearrange("l e h -> (l e) h")).then_inc(ld_rows, 16)
            sp.dma_start(rows[COL_B:COL_B1, :], ln_b.rearrange("l e h -> (l e) h")).then_inc(ld_rows, 16)
            sp.dma_start(rows[COL_B1:COL_QKV, :],
                         b1_dram.rearrange("l e (c p) -> (l e c) p", p=P)).then_inc(ld_rows, 16)
            sp.dma_start(rows[COL_QKV:NCOL, :],
                         in_proj_b.rearrange("(c p) -> c p", p=P)).then_inc(ld_rows, 16)

            def load_w1(l):
                sp.dma_start(w1_raw[:, l], w1_dram[l].rearrange("e p f -> p e f")).then_inc(ld_w1[l], 16)

            load_w1(0)
            for g in range(1, NG):
                load_x(g)
            for l in range(1, L):
                load_w1(l)
            for g in range(NG):
                sp.wait_ge(dve_final, g + 1)
                sp.dma_start(out_v[:, g * GT:(g + 1) * GT, :],
                             x_in[:, g * GT:(g + 1) * GT, :]).then_inc(st_out, 16)
            sp.wait_ge(st_out, 16 * NG)

        @block.scalar
        def _(act):
            own = Own(act, act_seq)
            act.dma_start(rw[:, 0:L * E], router_w.rearrange("l h e -> h l e")).then_inc(ld_small, 16)
            act.dma_start(rb[:, 0:L * E],
                          router_b.rearrange("l e -> (l e)").partition_broadcast(P)).then_inc(ld_small, 16)
            act.dma_start(b2[:, 0:L, :], b2_dram.rearrange("l e h -> e l h")).then_inc(ld_small, 16)
            act.dma_start(ob[:], out_b.unsqueeze(0)).then_inc(ld_small, 16)

            def load_w2(l):
                act.dma_start(w2_raw[:, l].rearrange("p e (c h) -> p e c h", h=D),
                              w2_dram[l].rearrange("e (c p) h -> p e c h", p=P)).then_inc(ld_w2[l], 16)

            load_w2(0)
            act.dma_start(proj[:, 0:3, :], in_proj_w.rearrange("(c p) h -> p c h", p=P)).then_inc(ld_proj, 16)
            act.dma_start(proj[:, 3, :], out_w).then_inc(ld_proj, 16)
            for l in range(1, L):
                load_w2(l)
            for f in range(FC):
                act.sem_inc(act_h[f], 1)

            def first_norm(g):
                tiles = range(g * GT, (g + 1) * GT)
                for t in tiles:
                    own(nc.scalar.activation(state[:, t], x_in[:, t], ACT.Identity, bias=nmean0[:, t:t + 1]))
                own.wait()
                for t in tiles:
                    ins = nc.scalar.activation(state[:, t], state[:, t], ACT.Identity, scale=rsd0[:, t:t + 1])
                    own(ins, act_xn0) if t == tiles[-1] else own(ins)

            def weigh(n2):
                act.wait_ge(dve_arg, n2)
                nc.scalar.activation(th[:], arg[:], ACT.Tanh).then_inc(act_th, 1)

            def keep_xbT(b2_):
                act.wait_ge(pe_row, b2_)
                nc.scalar.copy(xbT[:], t_ps[:, S:2 * S]).then_inc(act_xbT, 1)

            def keep_kv(b2_, s):
                act.wait_ge(pe_kv, b2_)
                nc.scalar.activation(kT[s][:], t_ps[:, 0:S], ACT.Identity,
                                     bias=cols[:, COL_QKV + 1:COL_QKV + 2])
                nc.scalar.copy(v[s][:].rearrange("p t h -> p (t h)"), t_ps[:, S:2 * S]).then_inc(act_kv, 1)

            def keep_res(b1):
                act.wait_ge(pe_res, b1)
                nc.scalar.copy(res[0:SEL, :], a_ps[0:SEL, 0:D]).then_inc(act_res, 1)

            def exponentials(b1):
                act.wait_ge(dve_mx, b1)
                for c in range(CH):
                    ins = nc.scalar.activation(
                        prob[0:QC, c, :], (a_ps, m_ps)[c // 2][0:QC, (c % 2) * S:(c % 2 + 1) * S], ACT.Exp,
                        bias=nmx[0:QC, c:c + 1], scale=SCALE, accum_out=den[0:QC, c:c + 1])
                ins.then_inc(act_exp, 1)

            def keep_pT(b1):
                act.wait_ge(pe_pT, b1)
                nc.scalar.copy(pT[:, 1, :], m_ps[:, 0:NH * TOP]).then_inc(act_pT, 1)

            def layers(first, last, attend):
                with act.Fori(first, last) as l:
                    act.wait_ge(pool_bias, nc.scalar.snap(l + 1))
                    with act.Fori(0, NG // 2) as i:
                        for s in range(2):
                            step(l, i, s, attend)

            def step(l, i, s, attend):
                n = l * NG + i * 2 + s
                c = [nc.scalar.snap(n * E + k) for k in range(1, E + 1)]
                n2 = nc.scalar.snap(n + 2)
                if attend:
                    b1, b2_ = nc.scalar.snap(n - (NX - 1)), nc.scalar.snap(n - (NX - 2))
                for e in range(E):
                    for f in range(FC):
                        if f == 0:
                            act.wait_ge(pe_y, c[e])
                        act.wait_ge(pe_h[f], c[e])
                        nc.scalar.activation(
                            hid[e % 2][:, f, :], h_ps[f][:], ACT.Gelu,
                            bias=bias_l[:, e * FC + f:e * FC + f + 1],
                        ).then_inc(act_h[f], 1)
                    if attend and e == 0:
                        keep_xbT(b2_)
                        keep_res(b1)
                    if attend and e == 1:
                        keep_kv(b2_, 1 - s)
                    if attend and e == 2:
                        exponentials(b1)
                if attend:
                    keep_pT(b1)
                weigh(n2)

            act.wait_ge(dve_rsd0, 1)
            first_norm(0)
            weigh(1)
            act.wait_ge(dve_rsd0, 2)
            for g in range(1, NG):
                first_norm(g)
            layers(0, LX, False)
            keep_xbT(1)
            keep_kv(1, 0)
            layers(LX, L, True)
            keep_res(B + 1)

        @block.gpsimd
        def _(pool):
            own = Own(pool, pool_seq)

            def select(t, compare, fill, base, pattern, mult):
                return own(nc.gpsimd.affine_select(out=t, in_=t, compare_op=compare, fill=fill, base=base,
                                                   pattern=pattern, channel_multiplier=mult))

            own(nc.gpsimd.memset(ident[:], 0.0))
            own(nc.gpsimd.memset(ones[:], 1.0))
            own(nc.gpsimd.memset(before4[:], 0.0))
            own(nc.gpsimd.memset(before[:], 0.0))
            own(nc.gpsimd.memset(heads[:], 1.0))
            own(nc.gpsimd.memset(mean_col[:], 1.0 / S))
            own(nc.gpsimd.memset(top_row[:], 1.0))
            own(nc.gpsimd.memset(half[:], 0.5))
            own(nc.gpsimd.memset(rw[:, L * E:], 0.0))
            own(nc.gpsimd.memset(rb[:, L * E:], 0.0))
            own(nc.gpsimd.memset(b2[:, L, :], 0.0))
            own(nc.gpsimd.iota(slot[:], pattern=[[1, SEL]], base=0, channel_multiplier=0,
                               allow_small_or_imprecise_dtypes=True))
            own.wait()
            select(ident[:], ALU.not_equal, 1.0, 0, [[-1, P]], 1)
            select(before4[:], ALU.is_ge, 1.0, 0, [[-1, E], [1, E]], 0)
            select(before[:], ALU.is_ge, 1.0, 0, [[-P, TB], [1, S]], -1)
            select(heads[:], ALU.is_ge, 0.0, 0, [[-HD, NH], [0, TOP]], 1)
            own(nc.gpsimd.memset(top_row[:, TOP:SEL], 0.0))
            own.wait()
            select(heads[:], ALU.is_ge, 0.0, HD - 1, [[HD, NH], [0, TOP]], -1)
            own.wait()
            pool.sem_inc(pool_const, 1)

            def first_sd(g0, g1):
                cols_ = slice(g0 * GT, g1 * GT)
                nc.gpsimd.tensor_tensor(sd0[:, cols_], ve0[:, cols_], half[:, cols_], ALU.pow).then_inc(pool_sd0, 1)

            def exact_root(square, count):
                pool.wait_ge(dve_square, count)
                nc.gpsimd.tensor_tensor(root0[:], square[:], half[:, 0:GT], ALU.pow).then_inc(pool_root, 1)

            def keep_xn(g1, tile):
                pool.wait_ge(dve_setup, 1)
                pool.wait_ge(dve_xn, g1)
                nc.gpsimd.tensor_copy(xn_all[:, bass.ds(tile, GT), :], xn[:]).then_inc(pool_xn, 1)

            def take(tile, s):
                nc.gpsimd.tensor_copy(grp[s][:], state[:, bass.ds(tile, GT), :]).then_inc(pool_grp, 1)

            def deviation(n2):
                pool.wait_ge(dve_var, n2)
                nc.gpsimd.tensor_tensor(sd[:], ve[:], half[:, 0:GT], ALU.pow).then_inc(pool_sd, 1)

            def place_w2(l, e):
                nc.gpsimd.tensor_copy(w2[:, e].rearrange("p c h -> p (c h)"),
                                      w2_raw[:, bass.ds(l, 1), e].rearrange("p o f -> p (o f)")
                                      ).then_inc(pool_w2, 1)

            def place_bias(l):
                nc.gpsimd.tensor_copy(bias_l[:], bias1[:, bass.ds(l * (E * FC), E * FC)]).then_inc(pool_bias, 1)

            def store(c6, tile, s):
                pool.wait_ge(dve_y, c6)
                pool.sem_inc(pool_alone, 1)
                nc.gpsimd.tensor_copy(state[:, bass.ds(tile, GT), :], grp[s][:]).then_inc(pool_store, 1)

            def bring(row, s):
                nc.gpsimd.tensor_copy(xb[s][:], xn_all[:, bass.ds(row * TB, TB), :])
                nc.gpsimd.tensor_copy(ecol[s][:], norm[:, bass.ds(row * TB, TB)])
                nc.gpsimd.tensor_copy(
                    eb[s][:], norm[:, bass.ds(row * TB, TB)].unsqueeze(2).to_broadcast([P, TB, P])).then_inc(pool_row, 1)

            def step(l, i, s, attend):
                n = l * NG + i * 2 + s
                n1 = nc.gpsimd.snap(n + 1)
                n2 = nc.gpsimd.snap(n + 2)
                c6 = nc.gpsimd.snap(n * E + (E + 2))
                pool.wait_ge(dve_setup, 1)
                pool.wait_ge(pool_store, n1)
                take(nc.gpsimd.snap(((i * 2 + (s + 1)) % NG) * GT), 1 - s)
                deviation(n2)
                if attend:
                    row = nc.gpsimd.snap((n - (NX - 2)) % B)
                    pool.wait_ge(dve_setup, 1)
                    pool.wait_ge(pe_xq, nc.gpsimd.snap(n - (NX - 1)))
                    bring(row, s)
                else:
                    g1 = nc.gpsimd.snap(l * (NG // 2) + (i + 1))
                    if s == 0:
                        exact_root(var, nc.gpsimd.snap(l * NG + (i * 2 + 1)))
                    else:
                        keep_xn(g1, nc.gpsimd.snap(l * (NG // 2 * GT) + i * GT))
                        exact_root(norm2, n1)
                store(c6, nc.gpsimd.snap((i * 2 + s) * GT), s)

            def place_layer(l):
                pool.wait_ge(dve_setup, 1)
                pool.wait_ge(act_h[FC - 1], nc.gpsimd.snap(l * (NG * E) + 1))
                pool.wait_ge(dve_b1, 2)
                place_bias(l)
                for e in range(E):
                    pool.wait_ge(dve_setup, 1)
                    pool.wait_ge(pe_y, nc.gpsimd.snap(l * (NG * E) + (e - E + 3)))
                    place_w2(l, e)

            def layers(first, last, attend):
                with pool.Fori(first, last) as l:
                    if first > 0:
                        place_layer(l)
                    with pool.Fori(0, NG // 2) as i:
                        for s in range(2):
                            step(l, i, s, attend)

            pool.wait_ge(dve_var0, 1)
            first_sd(0, 1)
            pool.wait_ge(act_xn0, 1)
            take(0, 0)
            deviation(1)
            pool.wait_ge(dve_var0, 2)
            first_sd(1, NG)
            pool.wait_ge(ld_w2[0], 16)
            for e in range(E):
                place_w2(0, e)
            pool.wait_ge(dve_b1, 1)
            place_bias(0)
            pool.sem_inc(pool_store, 1)
            pool.wait_ge(act_xn0, NG)
            layers(0, 1, False)
            for l in range(1, L):
                pool.wait_ge(ld_w2[l], 16)
            layers(1, LX, False)
            pool.wait_ge(pool_w2, LX * E)
            pool.wait_ge(pool_xn, NG)
            pool.wait_ge(dve_cx, 1)
            for s in range(2):
                bring(s, s)
            layers(LX, L, True)

        @block.vector
        def _(dve):
            V = nc.vector
            own = Own(dve, dve_seq)

            def wide(t, n, m=D):
                return t.unsqueeze(2).to_broadcast([P, n, m])

            def exact_variance(tile):
                xg = x_in[:, bass.ds(tile, GT), :]
                k = own(V.tensor_reduce(lane[:], xg.rearrange("p t (k l) -> p t l k", l=16), X, ALU.add))
                own.wait(k)
                l4 = lane[:].rearrange("p t (a b c) -> p t a b c", a=2, b=2)
                k = own(V.tensor_tensor(lane8[:], l4[:, :, :, 0], l4[:, :, :, 1], ALU.add))
                own.wait(k)
                k = own(V.tensor_tensor(lane4[:], lane8[:, :, 0], lane8[:, :, 1], ALU.add))
                own.wait(k)
                l2 = lane4[:].rearrange("p t (a b) -> p t a b", b=2)
                k = own(V.tensor_tensor(lane2[:], l2[:, :, :, 0], l2[:, :, :, 1], ALU.add))
                own.wait(k)
                k = own(V.tensor_tensor(mean[:], lane2[:, :, 0], lane2[:, :, 1], ALU.add))
                own.wait(k)
                k = own(V.tensor_scalar(mean[:], mean[:], 1.0 / D, None, ALU.mult))
                own.wait(k)
                k = own(V.tensor_tensor(dev[:], xg, wide(mean[:], GT), ALU.subtract))
                own.wait(k)
                k = own(V.tensor_tensor(rem[:], dev[:], dev[:], ALU.mult))
                windows(rem, vsum[:], k)
                own(V.tensor_scalar(var[:], vsum[:], 1.0 / D, EPS, ALU.mult, ALU.add), dve_square)

            def windows(t, out, k):
                own.wait(k)
                k = own(V.tensor_reduce(win[:], t[:].rearrange("p t (w k) -> p t w k", w=4), X, ALU.add))
                own.wait(k)
                k = own(V.tensor_reduce(out, win[:], X, ALU.add))
                own.wait(k)

            def exact_sqrt(out, a, y, t):
                y_hi, y_lo, hh, hl, ll, r, iy = t
                k1 = own(V.tensor_single_scalar(y_hi.bitcast(u32), y.bitcast(u32), HIGH, ALU.bitwise_and))
                own(V.reciprocal(iy, y))
                own.wait(k1)
                k2 = own(V.tensor_tensor(y_lo, y, y_hi, ALU.subtract))
                k3 = own(V.tensor_tensor(hh, y_hi, y_hi, ALU.mult))
                own.wait(k2)
                own(V.tensor_tensor(hl, y_hi, y_lo, ALU.mult))
                own(V.tensor_tensor(ll, y_lo, y_lo, ALU.mult))
                own.wait(k3)
                own(V.tensor_tensor(r, a, hh, ALU.subtract))
                own.wait()
                own(V.scalar_tensor_tensor(hh, hl, -2.0, r, ALU.mult, ALU.add))
                own.wait()
                own(V.tensor_tensor(r, hh, ll, ALU.subtract))
                own.wait()
                own(V.scalar_tensor_tensor(hl, r, 0.5, iy, ALU.mult, ALU.mult))
                own.wait()
                return own(V.tensor_tensor(out, y, hl, ALU.add))

            def exact_root(count):
                dve.wait_ge(pool_root, count)
                k = exact_sqrt(sd_x[:], var[:], root0[:], [t[:] for t in sqs])
                own.wait(k)
                k1 = own(V.tensor_single_scalar(sd_hi[:].bitcast(u32), sd_x[:].bitcast(u32), HIGH, ALU.bitwise_and))
                k2 = own(V.reciprocal(inv[:], sd_x[:]))
                own.wait(k1)
                own(V.tensor_tensor(sd_lo[:], sd_x[:], sd_hi[:], ALU.subtract))
                own.wait(k2)
                own(V.tensor_scalar(ninv[:], inv[:], -1.0, None, ALU.mult))
                k = own(V.tensor_tensor(q0[:], dev[:], wide(inv[:], GT), ALU.mult))
                own.wait(k)
                k = own(V.tensor_single_scalar(q_hi[:].bitcast(u32), q0[:].bitcast(u32), HIGH, ALU.bitwise_and))
                own.wait(k)
                own(V.tensor_tensor(q_lo[:], q0[:], q_hi[:], ALU.subtract))

            def exact_remainder():
                last = [None] * GT
                for q, sd_part, other in ((q_hi, sd_hi, dev), (q_hi, sd_lo, rem), (q_lo, sd_hi, rem),
                                          (q_lo, sd_lo, rem)):
                    for t in range(GT):
                        if last[t] is not None:
                            own.wait(last[t])
                        last[t] = own(V.scalar_tensor_tensor(
                            rem[:, t], q[:, t], sd_part[:, t:t + 1], other[:, t], ALU.mult,
                            ALU.subtract if other is dev else ALU.add))

            def exact_quotient(g1):
                own.wait()
                for t in range(GT):
                    ins = V.scalar_tensor_tensor(xn[:, t], rem[:, t], ninv[:, t:t + 1], q0[:, t],
                                                 ALU.mult, ALU.add)
                    own(ins, dve_xn) if t == GT - 1 else own(ins)
                dve.wait_ge(dve_xn, g1)
                k = own(V.tensor_tensor(rem[:], xn[:], xn[:], ALU.mult))
                own.wait(k)
                k = own(V.tensor_reduce(win[:], rem[:].rearrange("p t (w k) -> p t w k", w=4), X, ALU.add))
                own.wait(k)
                own(V.tensor_reduce(norm2[:], win[:], X, ALU.add), dve_square)

            def exact_norm(count, tile):
                dve.wait_ge(pool_root, count)
                exact_sqrt(norm[:, bass.ds(tile, GT)], norm2[:], root0[:], [t[:] for t in sqs])

            def place_w1(l, e):
                w1_g = w1_gs[e % 2]
                own(V.tensor_scalar(w1_g[:], w1_raw[:, bass.ds(l, 1), e].rearrange("p o f -> p (o f)"),
                                    cols[:, bass.ds(l * E + (COL_G + e), 1)], None, ALU.mult))
                own.wait()
                own(V.tensor_copy(w1_hi[:, e], w1_g[:]))
                own.wait()
                own(V.tensor_tensor(w1_lo[:, e], w1_g[:], w1_hi[:, e].bitcast(fp32), ALU.subtract), dve_w1)

            def group_stats(s, n2):
                dve.wait_ge(pool_grp, n2)
                for t in range(GT):
                    own(V.bn_stats(stats[:, t], grp[s][:, t]))
                own.wait()
                for t in range(GT):
                    own(V.bn_aggr(mv[:, t], stats[:, t]))
                own.wait()
                own(V.tensor_scalar(ve[:], mv[:, :, 1], EPS, None, ALU.add), dve_var)

            def normalise(s, n1, n2):
                dve.wait_ge(pool_sd, n2)
                own(V.reciprocal(rsd[:], sd[:]))
                own.wait()
                if n1 is not None:
                    dve.wait_ge(pe_xT, n1)
                for t in range(GT):
                    ins = V.tensor_scalar(xhat[:, t], grp[s][:, t], mv[:, t, 0:1], rsd[:, t:t + 1],
                                          ALU.subtract, ALU.mult)
                    own(ins, dve_xhat) if t == GT - 1 else own(ins)

            def split_xT(s, n2):
                dve.wait_ge(pe_xT, n2)
                own(V.tensor_copy(xT_hi[s][:], t_ps[:]))
                own.wait()
                own(V.tensor_tensor(xT_lo[s][:], t_ps[:], xT_hi[s][:].bitcast(fp32), ALU.subtract), dve_xT)

            def rank_experts(s, n2, col):
                def over(t):
                    return t[:, bass.ds(col, E)].unsqueeze(1).to_broadcast([P, GT, E])

                own(V.tensor_tensor(lg_a[:], over(rw_sum), wide(mv[:, :, 0], GT, E), ALU.mult))
                own.wait()
                own(V.tensor_tensor(lg_a[:], lg_a[:], over(rb), ALU.add))
                dve.wait_ge(pe_lg, n2)
                own(V.tensor_tensor(lg[:], m_ps[:, 0:GT * E].rearrange("p (t e) -> p t e", e=E),
                                    wide(sd[:], GT, E), ALU.mult))
                own.wait()
                own(V.tensor_tensor(lg[:], lg[:], lg_a[:], ALU.add))
                own.wait()
                mine = lg[:].unsqueeze(3).to_broadcast([P, GT, E, E])
                other = lg[:].unsqueeze(2).to_broadcast([P, GT, E, E])
                own(V.tensor_tensor(cmp_eq[:], other, mine, ALU.is_equal))
                own(V.tensor_tensor(cmp_gt[:], other, mine, ALU.is_gt))
                own.wait(own.n - 1)
                own(V.tensor_tensor(cmp_eq[:], cmp_eq[:],
                                    before4[:].unsqueeze(1).to_broadcast([P, GT, E, E]), ALU.mult))
                own.wait()
                own(V.tensor_tensor(cmp_gt[:], cmp_gt[:], cmp_eq[:], ALU.add))
                own.wait()
                own(V.tensor_reduce(place[:], cmp_gt[:], X, ALU.add))
                own.wait()
                own(V.tensor_scalar(chosen[:], place[:], K_TOP - 0.5, None, ALU.is_lt))
                own.wait()
                own(V.tensor_tensor(lg_a[:], lg[:], chosen[:], ALU.mult))
                own.wait()
                own(V.tensor_reduce(two[:], lg_a[:], X, ALU.add))
                own.wait()
                own(V.scalar_tensor_tensor(arg[:], wide(two[:], GT, E), -0.5, lg[:], ALU.mult, ALU.add), dve_arg)

            def combine(s, n2):
                dve.wait_ge(act_th, n2)
                own(V.tensor_scalar(th[:], th[:], 0.5, 0.5, ALU.mult, ALU.add))
                own.wait()
                own(V.tensor_tensor(comb[s][:], th[:], chosen[:], ALU.mult), dve_comb)

            def keep_combT(n2):
                dve.wait_ge(pe_combT, n2)
                own(V.tensor_copy(combT[:], m_ps[0:E, :]), dve_combT)

            def add_z(s, n1):
                dve.wait_ge(pe_z, n1)
                own(V.tensor_tensor(grp[s][:], m_ps[:].rearrange("p (t h) -> p t h", h=D), grp[s][:],
                                    ALU.add), dve_z)
                own.wait()

            def add_y(s, e, c3):
                dve.wait_ge(pe_y, c3)
                own.wait()
                for t in range(GT):
                    ins = V.scalar_tensor_tensor(grp[s][:, t], y_ps[e % 2][:, t * D:(t + 1) * D],
                                                 comb[s][:, t, e:e + 1], grp[s][:, t], ALU.mult, ALU.add)
                    own(ins, dve_y) if t == GT - 1 else own(ins)

            def rank_tokens(b2_, s):
                dve.wait_ge(act_xbT, b2_)
                for a in range(TB):
                    e_a = ecol[s][:, a:a + 1]
                    own(V.tensor_scalar(gt_out[:], t_ps[:, 0:S], e_a, None, ALU.is_gt, ALU.add,
                                        accum_out=n_gt[:, a:a + 1]))
                    own(V.scalar_tensor_tensor(eq_out[:], t_ps[:, 0:S], e_a, before[:, a], ALU.is_equal,
                                               ALU.mult, accum_out=n_eq[:, a:a + 1]))
                    own.wait()
                own(V.tensor_tensor(rank[:], n_gt[:], n_eq[:], ALU.add))
                own.wait()
                own(V.tensor_scalar(rank[:], rank[:], float(TOP), None, ALU.min))
                own.wait()
                own(V.tensor_tensor(onehot[:], slot[:].unsqueeze(1).to_broadcast([P, TB, SEL]),
                                    wide(rank[:], TB, SEL), ALU.is_equal), dve_onehot)

            def keep_xq(b2_, s):
                dve.wait_ge(pe_xq, b2_)
                own(V.tensor_copy(xqT[:], t_ps[:, 0:SEL]))
                own(V.tensor_copy(meanT[s][:, TOP:SEL], t_ps[:, SEL:SEL + 1]))
                own(V.tensor_copy(onehotT[s][0:SEL, :], t_ps[0:SEL, P:P + S]), dve_xq)

            def spread_q(b2_, s):
                dve.wait_ge(pe_q, b2_)
                own(V.tensor_scalar(qT[:, 0:TOP], t_ps[:, 0:TOP], cols[:, COL_QKV:COL_QKV + 1], None, ALU.add))
                own.wait()
                own(V.tensor_tensor(qbd[s][:], qT[:, 0:TOP].unsqueeze(1).to_broadcast([P, NH, TOP]),
                                    heads[:], ALU.mult), dve_qbd)

            def maxima(b1):
                dve.wait_ge(pe_sc, b1)
                for c, ps in enumerate((a_ps, m_ps)):
                    own(V.tensor_reduce(mx[0:QC, 2 * c:2 * c + 2],
                                        ps[0:QC, :].rearrange("p (c s) -> p c s", s=S), X, ALU.max))
                own.wait()
                own(V.tensor_scalar(nmx[0:QC, :], mx[0:QC, :], -SCALE, None, ALU.mult), dve_mx)

            def probabilities(b1):
                dve.wait_ge(act_exp, b1)
                own(V.reciprocal(rden[0:QC, :], den[0:QC, :]))
                own.wait()
                for c in range(CH):
                    ins = V.tensor_scalar(prob[0:QC, c], prob[0:QC, c], rden[0:QC, c:c + 1], None, ALU.mult)
                    own(ins, dve_prob) if c == CH - 1 else own(ins)

            def keep_pT(b1):
                dve.wait_ge(pe_pT, b1)
                own(V.tensor_copy(pT[:, 0, :], a_ps[:, 0:NH * TOP]), dve_pT)

            def pick_heads(b1):
                dve.wait_ge(pe_cx, b1)
                own(V.tensor_tensor(picked[:], a_ps[:, 0:NH * TOP].rearrange("p (h q) -> p h q", q=TOP),
                                    heads[:], ALU.mult))
                own.wait()
                own(V.tensor_reduce(cx[:], picked[:].rearrange("p h q -> p q h"), X, ALU.add))
                own.wait()
                own(V.tensor_scalar(ctxT[:, 0:TOP], cx[:], cols[:, COL_QKV + 2:COL_QKV + 3], None,
                                    ALU.add), dve_cx)

            def add_attention(b1, tile):
                dve.wait_ge(pe_out, b1)
                own(V.tensor_tensor(x_in[:, bass.ds(tile, TB), :],
                                    a_ps[:, 0:TB * D].rearrange("p (t h) -> p t h", h=D),
                                    x_in[:, bass.ds(tile, TB), :], ALU.add), dve_out)

            def first_stats(g):
                dve.wait_ge(ld_x[g], 16)
                own.wait()
                for t in range(GT):
                    own(V.bn_stats(stats0[:, t], x_in[:, g * GT + t]))
                own.wait()
                for t in range(GT):
                    own(V.bn_aggr(mv0[:, g * GT + t], stats0[:, t]))

            def first_variance(g0, g1):
                own.wait()
                own(V.tensor_scalar(ve0[:, g0 * GT:g1 * GT], mv0[:, g0 * GT:g1 * GT, 1], EPS, None, ALU.add),
                    dve_var0)

            def first_deviation(g0, g1):
                own(V.tensor_scalar(nmean0[:, g0 * GT:g1 * GT], mv0[:, g0 * GT:g1 * GT, 0], -1.0, None, ALU.mult))
                own.wait()
                own(V.reciprocal(rsd0[:, g0 * GT:g1 * GT], sd0[:, g0 * GT:g1 * GT]), dve_rsd0)

            first_stats(0)
            first_variance(0, 1)
            dve.wait_ge(pe_setup, 1)
            own(V.tensor_copy(cols[:], t_ps[:, 0:NCOL]))
            dve.wait_ge(pool_sd0, 1)
            first_deviation(0, 1)
            dve.wait_ge(pe_setup, 2)
            own(V.tensor_copy(rw_sum[:], y_ps[0][:, 0:LE1]))
            own(V.tensor_copy(rw_hi[:], rw[:]))
            own.wait()
            own(V.tensor_tensor(rw_lo[:], rw[:], rw_hi[:].bitcast(fp32), ALU.subtract), dve_setup)
            group_stats(0, 1)
            dve.wait_ge(ld_w1[0], 16)
            place_w1(0, 0)
            normalise(0, None, 1)
            for g in range(1, NG):
                first_stats(g)
                if g == 2:
                    split_xT(0, 1)
            first_variance(1, NG)
            rank_experts(0, 1, 0)
            place_w1(0, 1)
            combine(0, 1)
            dve.wait_ge(pool_sd0, 2)
            first_deviation(1, NG)
            dve.wait_ge(pe_b1, 1)
            own(V.tensor_tensor(bias1[:, 0:E * FC], a_ps[:, 0:E * FC], cols[:, COL_B1:COL_B1 + E * FC], ALU.add),
                dve_b1)
            for e in range(2, E):
                place_w1(0, e)
            dve.wait_ge(pe_setup, 3)
            own(V.tensor_copy(projT[:].rearrange("p c h -> p (c h)"), a_ps[:]))
            own.wait()
            dve.sem_inc(dve_y, 2)

            def step(l, i, s, attend):
                n = l * NG + i * 2 + s
                c = {k: V.snap(n * E + k) for k in range(3, E + 3)}
                n1, n2 = V.snap(n + 1), V.snap(n + 2)
                g_tile = l * (NG // 2 * GT) + i * GT
                if attend:
                    b1, b2_ = V.snap(n - (NX - 1)), V.snap(n - (NX - 2))
                keep_combT(n1)
                if attend:
                    rank_tokens(b2_, 1 - s)
                add_z(s, n1)
                if attend:
                    add_attention(b1, V.snap(((n - (NX - B + 1)) % B) * TB))
                group_stats(1 - s, n2)
                if not attend and s == 0:
                    exact_variance(V.snap(g_tile))
                add_y(s, 0, c[3])
                normalise(1 - s, n1, n2)
                if attend:
                    maxima(b1)
                elif s == 0:
                    exact_root(n1)
                else:
                    exact_remainder()
                add_y(s, 1, c[4])
                split_xT(1 - s, n2)
                if attend:
                    probabilities(b1)
                elif s == 1:
                    exact_quotient(V.snap(l * (NG // 2) + (i + 1)))
                if attend:
                    keep_pT(b1)
                    keep_xq(b2_, 1 - s)
                add_y(s, 2, c[5])
                rank_experts(1 - s, n2, V.snap(((n + 1) // NG) * E))
                if attend:
                    spread_q(b2_, 1 - s)
                    pick_heads(b1)
                combine(1 - s, n2)
                if not attend and s == 1:
                    exact_norm(n1, V.snap(g_tile))
                add_y(s, 3, c[6])
                own.clear()

            def layers(first, last, attend):
                own.clear()
                with dve.Fori(first, last) as l:
                    if first > 0:
                        for e in range(E):
                            place_w1(l, e)
                        own.clear()
                    with dve.Fori(0, NG // 2) as i:
                        for s in range(2):
                            step(l, i, s, attend)

            layers(0, 1, False)
            dve.wait_ge(pe_b1, 2)
            own(V.tensor_tensor(bias1[:, E * FC:], a_ps[:, 0:NB1 - E * FC], cols[:, COL_B1 + E * FC:COL_QKV],
                                ALU.add), dve_b1)
            for l in range(1, L):
                dve.wait_ge(ld_w1[l], 16)
            layers(1, LX, False)
            dve.wait_ge(pool_w2, LX * E)
            for t in (onehotT[1], meanT[0], meanT[1], mx):
                own(V.memset(t[:], 0.0))
            own(V.memset(ctxT[:], 0.0), dve_cx)
            dve.wait_ge(dve_cx, 1)
            rank_tokens(1, 0)
            keep_xq(1, 0)
            spread_q(1, 0)
            layers(LX, L, True)
            add_attention(B + 1, (B - 1) * TB)
            dve.wait_ge(dve_out, B + 1)
            dve.wait_ge(pool_store, NX * L // LX + 1)
            for g in range(NG):
                own(V.tensor_tensor(x_in[:, g * GT:(g + 1) * GT, :], x_in[:, g * GT:(g + 1) * GT, :],
                                    state[:, g * GT:(g + 1) * GT, :], ALU.add), dve_final)

        @block.tensor
        def _(pe):
            T = nc.tensor
            pe.wait_ge(pool_const, 1)
            pe.wait_ge(ld_rows, 64)
            T.transpose(t_ps[:, 0:NCOL], rows[0:NCOL, :], ident[0:NCOL, 0:NCOL]).then_inc(pe_setup, 1)
            pe.wait_ge(ld_small, 64)
            T.matmul(y_ps[0][:, 0:LE1], ones[:], rw[:], start=True, stop=True).then_inc(pe_setup, 1)
            pe.wait_ge(dve_setup, 1)

            def transpose_x(n2, n1, b2_=None):
                pe.wait_ge(dve_xhat, n2)
                if n1 is not None:
                    pe.wait_ge(dve_xT, n1)
                if b2_ is not None:
                    pe.wait_ge(act_kv, b2_)
                for t in range(GT):
                    ins = T.transpose(t_ps[:, t * P:(t + 1) * P], xhat[:, t], ident[:])
                ins.then_inc(pe_xT, 1)

            def route(s, n2, n1, col, b1=None):
                pe.wait_ge(dve_xT, n2)
                if n1 is not None:
                    pe.wait_ge(dve_z, n1)
                if b1 is not None:
                    pe.wait_ge(act_pT, b1)
                for t in range(GT):
                    o = m_ps[:, t * E:(t + 1) * E]
                    hi, lo = (x[s][:, t * P:(t + 1) * P] for x in (xT_hi, xT_lo))
                    T.matmul(o, hi, rw_hi[:, bass.ds(col, E)], start=True, stop=False)
                    T.matmul(o, hi, rw_lo[:, bass.ds(col, E)], start=False, stop=False)
                    ins = T.matmul(o, lo, rw_hi[:, bass.ds(col, E)], start=False, stop=True)
                ins.then_inc(pe_lg, 1)

            def transpose_comb(s, n2):
                pe.wait_ge(dve_comb, n2)
                for t in range(GT):
                    ins = T.transpose(m_ps[0:E, t * P:(t + 1) * P], comb[s][:, t], ident[:])
                ins.then_inc(pe_combT, 1)

            def second_bias(n1, l):
                pe.wait_ge(pool_const, 1)
                pe.wait_ge(dve_combT, n1)
                for t in range(GT):
                    ins = T.matmul(m_ps[:, t * D:(t + 1) * D], combT[:, t * P:(t + 1) * P],
                                   b2[:, bass.ds(l, 1), :].rearrange("e o h -> e (o h)"), start=True, stop=True)
                ins.then_inc(pe_z, 1)

            def hidden(s, e, c, c1, w):
                pe.wait_ge(dve_w1, w)
                for f in range(FC):
                    if f == 0:
                        pe.wait_ge(act_h[FC - 1], c)
                    elif f == FC - 1:
                        pe.wait_ge(act_h[0], c1)
                    else:
                        pe.wait_ge(act_h[f], c)
                    hi, lo = (x[:, e, f * P:(f + 1) * P] for x in (w1_hi, w1_lo))
                    T.matmul(h_ps[f][:], hi, xT_hi[s][:], start=True, stop=False)
                    T.matmul(h_ps[f][:], hi, xT_lo[s][:], start=False, stop=False)
                    T.matmul(h_ps[f][:], lo, xT_hi[s][:], start=False, stop=True).then_inc(pe_h[f], 1)

            def outputs(e, c1, c2, w):
                pe.wait_ge(dve_y, c1)
                pe.wait_ge(pool_w2, w)
                for t in range(GT):
                    for f in range(FC):
                        if t == 0:
                            pe.wait_ge(act_h[f], c2)
                        ins = T.matmul(y_ps[e % 2][:, t * D:(t + 1) * D], hid[e % 2][:, f, t * P:(t + 1) * P],
                                       w2[:, e, f], start=(f == 0), stop=(f == FC - 1))
                ins.then_inc(pe_y, 1)

            def row_first(b2_, s):
                pe.wait_ge(pool_row, b2_)
                for a in range(TB):
                    T.transpose(t_ps[:, a * P:(a + 1) * P], eb[s][:, a], ident[:])
                for a in range(TB):
                    ins = T.transpose(t_ps[:, S + a * P:S + (a + 1) * P], xb[s][:, a], ident[:])
                ins.then_inc(pe_row, 1)

            def row_kv(b2_):
                pe.wait_ge(act_xbT, b2_)
                pe.wait_ge(dve_onehot, b2_)
                T.matmul(t_ps[:, 0:S], projT[:, 1], xbT[:], start=True, stop=True)
                for a in range(TB):
                    ins = T.matmul(t_ps[:, S + a * D:S + (a + 1) * D], xbT[:, a * P:(a + 1) * P],
                                   projT[:, 2], start=True, stop=True)
                ins.then_inc(pe_kv, 1)

            def row_select(s):
                for a in range(TB):
                    T.transpose(t_ps[0:SEL, (1 + a) * P:(2 + a) * P], onehot[:, a], ident[:])
                for a in range(TB):
                    T.matmul(t_ps[:, 0:SEL], xb[s][:, a], onehot[:, a], start=(a == 0), stop=(a == TB - 1))
                for a in range(TB):
                    ins = T.matmul(t_ps[:, SEL:SEL + 1], xb[s][:, a], mean_col[:], start=(a == 0), stop=(a == TB - 1))
                ins.then_inc(pe_xq, 1)

            def row_q(b2_):
                pe.wait_ge(dve_xq, b2_)
                T.matmul(t_ps[:, 0:SEL], projT[:, 0], xqT[:], start=True, stop=True).then_inc(pe_q, 1)

            def row_scores(s):
                for c in range(CH):
                    ins = T.matmul(
                        (a_ps, m_ps)[c // 2][0:QC, (c % 2) * S:(c % 2 + 1) * S],
                        qbd[s][:].rearrange("p h q -> p (h q)")[:, c * QC:(c + 1) * QC], kT[s][:],
                        start=True, stop=True)
                ins.then_inc(pe_sc, 1)

            def transpose_prob(b1):
                pe.wait_ge(dve_prob, b1)
                for a, ps in enumerate((a_ps, m_ps)):
                    for c in range(CH):
                        ins = T.transpose(ps[:, c * QC:(c + 1) * QC], prob[0:QC, c, a * P:(a + 1) * P],
                                          ident[0:QC, 0:QC])
                ins.then_inc(pe_pT, 1)

            def contexts(b1, s):
                pe.wait_ge(dve_pT, b1)
                T.matmul(a_ps[:, 0:NH * TOP], v[s][:, 0], pT[:, 0], start=True, stop=False)
                pe.wait_ge(act_pT, b1)
                T.matmul(a_ps[:, 0:NH * TOP], v[s][:, 1], pT[:, 1], start=False, stop=True).then_inc(pe_cx, 1)

            def results(b1, s):
                T.matmul(a_ps[0:SEL, 0:D], meanT[s][:], ident[:], start=True, stop=False)
                T.matmul(a_ps[0:SEL, 0:D], top_row[:], ob[:], start=False, stop=False)
                T.matmul(a_ps[0:SEL, 0:D], ctxT[:], projT[:, 3], start=False, stop=True).then_inc(pe_res, 1)

            def spread_results(b1, s):
                pe.wait_ge(act_res, b1)
                for a in range(TB):
                    ins = T.matmul(a_ps[:, a * D:(a + 1) * D], onehotT[s][0:SEL, a * P:(a + 1) * P],
                                   res[0:SEL, :], start=True, stop=True)
                ins.then_inc(pe_out, 1)

            def first_biases(ms):
                for j, m in enumerate(ms):
                    for f in range(FC):
                        ins = T.matmul(a_ps[:, j * FC + f:j * FC + f + 1], w1_raw[:, m // E, m % E, f * P:(f + 1) * P],
                                       cols[:, COL_B + m:COL_B + m + 1], start=True, stop=True)
                ins.then_inc(pe_b1, 1)

            def step(l, i, s, w, attend):
                n = l * NG + i * 2 + s
                c = {k: T.snap(n * E + k) for k in range(1, E + 2)}
                n1, n2 = T.snap(n + 1), T.snap(n + 2)
                if attend:
                    b1, b2_ = T.snap(n - (NX - 1)), T.snap(n - (NX - 2))
                hidden(s, 0, c[1], c[2], w[0])
                transpose_comb(s, n1)
                if attend:
                    pe.wait_ge(dve_qbd, b1)
                    row_first(b2_, 1 - s)
                    pe.wait_ge(dve_cx, b1)
                    results(b1, 1 - s)
                hidden(s, 1, c[2], c[3], w[1])
                second_bias(n1, l)
                if attend:
                    spread_results(b1, 1 - s)
                outputs(0, c[1], c[2], w[0])
                if attend:
                    pe.wait_ge(dve_out, b1)
                    pe.wait_ge(dve_z, n1)
                    row_scores(s)
                    row_kv(b2_)
                hidden(s, 2, c[3], c[4], w[2])
                outputs(1, c[2], c[3], w[1])
                transpose_x(n2, n1, b2_ if attend else None)
                hidden(s, 3, c[4], c[5], w[3])
                if attend:
                    transpose_prob(b1)
                    pe.wait_ge(dve_xT, n2)
                    row_select(1 - s)
                outputs(2, c[3], c[4], w[2])
                route(1 - s, n2, n1, T.snap(((n + 1) // NG) * E), b1 if attend else None)
                if attend:
                    row_q(b2_)
                    contexts(b1, s)
                outputs(3, c[4], c[5], w[3])

            def layers(first, last, attend):
                with pe.Fori(first, last) as l:
                    w = [T.snap(l * E + (e + 1)) for e in range(E)]
                    with pe.Fori(0, NG // 2) as i:
                        for s in range(2):
                            step(l, i, s, w, attend)

            transpose_x(1, None)
            pe.wait_ge(ld_w1[0], 16)
            first_biases(range(E))
            route(0, 1, None, 0)
            pe.wait_ge(ld_proj, 32)
            pe.wait_ge(dve_b1, 1)
            for c in range(4):
                ins = T.transpose(a_ps[:, c * D:(c + 1) * D], proj[:, c, :], ident[:])
            ins.then_inc(pe_setup, 1)
            pe.sem_inc(pe_y, 2)
            pe.wait_ge(dve_w1, E)
            layers(0, 1, False)
            for l in range(1, L):
                pe.wait_ge(ld_w1[l], 16)
            first_biases(range(E, L * E))
            layers(1, LX, False)
            row_first(1, 0)
            row_kv(1)
            pe.wait_ge(act_kv, 1)
            row_select(0)
            row_q(1)
            layers(LX, L, True)
            pe.wait_ge(dve_cx, B + 1)
            results(B + 1, 1)
            spread_results(B + 1, 1)


_INS = ["L0_attn_x", "L0_attn_in_proj_w", "L0_attn_in_proj_b", "L0_attn_out_w", "L0_attn_out_b",
        "L0_ffn_router_w", "L0_ffn_router_b", "L0_ffn_ln_g", "L0_ffn_ln_b", "L0_ffn_w1", "L0_ffn_b1",
        "L0_ffn_w2", "L0_ffn_b2"]


def kernel(**inputs):
    import numpy as _np
    import concourse.bacc as _bacc
    from concourse import mybir as _mybir
    from concourse.bass_utils import run_bass_kernel_spmd as _run

    nc = _bacc.Bacc("TRN2", target_bir_lowering=False, num_devices=1)
    arrays, args = {}, []
    for name in _INS:
        a = _np.ascontiguousarray(inputs[name])
        arrays[f"in_{name}"] = a
        args.append(nc.dram_tensor(f"in_{name}", a.shape, _mybir.dt.from_np(a.dtype), kind="ExternalInput").ap())
    shape = inputs["L0_attn_x"].shape
    args.append(nc.dram_tensor("out", shape, _mybir.dt.float32, kind="ExternalOutput").ap())
    attention_and_experts_kernel(nc, *args)
    r = _run(nc, [arrays], core_ids=[0])
    return r.results[0]["out"]
```

```python
import concourse.bass as bass
from concourse import mybir
from contextlib import ExitStack


def attention_and_experts_kernel(
    nc: bass.Bass,
    x_dram: bass.AP,
    in_proj_w: bass.AP,
    in_proj_b: bass.AP,
    out_w: bass.AP,
    out_b: bass.AP,
    router_w: bass.AP,
    router_b: bass.AP,
    ln_g: bass.AP,
    ln_b: bass.AP,
    w1_dram: bass.AP,
    b1_dram: bass.AP,
    w2_dram: bass.AP,
    b2_dram: bass.AP,
    out_dram: bass.AP,
):
    fp32 = mybir.dt.float32
    fp32r = mybir.dt.float32r
    u32 = mybir.dt.uint32
    ALU = mybir.AluOpType
    ACT = mybir.ActivationFunctionType
    X = mybir.AxisListType.X

    B, S, D = x_dram.shape
    P = 128
    TB = S // P
    NT = B * TB
    L, E, _, F = w1_dram.shape
    FC = F // P
    GT = 4
    NG = NT // GT
    GN = GT * P
    EPS = 1e-5
    NH = 16
    HD = D // NH
    TOP = 27
    SEL = TOP + 1
    CH = 4
    HC = NH // CH
    QC = HC * TOP
    SCALE = float(HD) ** -0.5
    HIGH = 0xFFFFF000
    K_TOP = 2
    LX = 2
    NX = LX * NG

    x_v = x_dram.rearrange("b (t p) h -> p (b t) h", p=P)
    out_v = out_dram.rearrange("b (t p) h -> p (b t) h", p=P)

    ctx = ExitStack()
    with ctx:
        def sb(name, shape, dt=fp32):
            return ctx.enter_context(nc.sbuf_tensor(name, shape, dt))

        def sem(name):
            return ctx.enter_context(nc.semaphore(name))

        x_in = sb("x_in", [P, NT, D])
        xn_all = sb("xn_all", [P, NT, D])
        state = sb("state", [P, NT, D])
        raw = sb("raw", [P, L * E * 2 * F])
        raw_v = raw[:].rearrange("p (l w e f) -> p l w e f", w=2, e=E, f=F)
        w1_raw = raw_v[:, :, 0]
        w2_raw = raw_v[:, :, 1]
        w1_hi = sb("w1_hi", [P, E, F], fp32r)
        w1_lo = sb("w1_lo", [P, E, F], fp32r)
        w1_gs = [sb(f"w1_g{i}", [P, F]) for i in range(2)]
        w2 = sb("w2", [P, E, FC, D])
        NB1 = L * E * FC
        COL_G, COL_B, COL_B1, COL_QKV = 0, L * E, 2 * L * E, 2 * L * E + NB1
        COL_OB = COL_QKV + 3
        NCOL = COL_OB + 1
        rows = sb("rows", [P, P])
        cols = sb("cols", [P, NCOL])
        ln_b_diag = sb("ln_b_diag", [P, L * E, L * E])
        bias_rows = sb("bias_rows", [L * E, F])
        bias1 = sb("bias1", [P, L * E, FC])
        bias_l = sb("bias_l", [P, E * FC])
        LE1 = (L + 1) * E
        rw = sb("rw", [P, LE1])
        rw_parts = sb("rw_parts", [P, L + 1, 2, E], fp32r)
        rb = sb("rb", [P, LE1])
        rw_sum = sb("rw_sum", [P, LE1])
        KB = 3 * E
        b2_parts = sb("b2_parts", [KB, L, D], fp32r)
        in_mid = sb("in_mid", [KB, 1])
        out_mid = sb("out_mid", [KB, 1])
        proj = sb("proj", [P, 4, D])
        projT = sb("projT", [P, 4, D])
        ident = sb("ident", [P, P])
        eye = sb("eye", [P, L * E, L * E])
        ones = sb("ones", [P, P])
        warm = sb("warm", [P, 1])
        before4 = sb("before4", [P, E, E])
        before = sb("before", [P, TB, S])
        slot = sb("slot", [P, SEL])
        heads = sb("heads", [P, NH, TOP])
        half = sb("half", [P, GT])
        grp = [sb(f"grp{i}", [P, GT, D]) for i in range(2)]
        xhat = sb("xhat", [P, GT, D])
        xT_hi = [sb(f"xT_hi{i}", [P, GN], fp32r) for i in range(2)]
        xT_lo = [sb(f"xT_lo{i}", [P, GN], fp32r) for i in range(2)]
        hid = [sb(f"hid{i}", [P, FC, GN]) for i in range(2)]
        stats = sb("stats", [P, GT, 6])
        mv = sb("mv", [P, GT, 2])
        ve = sb("ve", [P, GT])
        sd = sb("sd", [P, GT])
        rsd = sb("rsd", [P, GT])
        lg = sb("lg", [P, GT, E])
        lg_a = sb("lg_a", [P, GT, E])
        arg = sb("arg", [P, GT, E])
        th = sb("th", [P, GT, E])
        cmp_gt = sb("cmp_gt", [P, GT, E, E])
        cmp_eq = sb("cmp_eq", [P, GT, E, E])
        place = sb("place", [P, GT, E])
        chosen = sb("chosen", [P, GT, E])
        two = sb("two", [P, GT])
        comb = [sb(f"comb{i}", [P, GT, E]) for i in range(2)]
        comb_parts = [sb(f"comb_parts{i}", [P, GT, 3, E]) for i in range(2)]
        combT = sb("combT", [KB, GN], fp32r)
        stats0 = sb("stats0", [P, GT, 6])
        mv0 = sb("mv0", [P, GT, 2])
        ve0 = sb("ve0", [P, GT])
        sd0 = sb("sd0", [P, GT])
        rsd0 = sb("rsd0", [P, GT])
        nmean0 = sb("nmean0", [P, GT])
        x_dev = sb("x_dev", [P, GT, D])
        lane = sb("lane", [P, GT, 16])
        lane8 = sb("lane8", [P, GT, 2, 4])
        lane4 = sb("lane4", [P, GT, 4])
        lane2 = sb("lane2", [P, GT, 2])
        mean = sb("mean", [P, GT])
        dev = sb("dev", [P, GT, D])
        q0 = sb("q0", [P, GT, D])
        q_hi = sb("q_hi", [P, GT, D])
        b2, b2_hi, b2_lo = (t[0:KB, 0:L, :] for t in (dev, q0, q_hi))
        q_lo = sb("q_lo", [P, GT, D])
        rem = sb("rem", [P, GT, D])
        xn = sb("xn", [P, GT, D])
        win = sb("win", [P, GT, 4])
        vsum = sb("vsum", [P, GT])
        var = sb("var", [P, GT])
        sqs = [sb(f"sqs{i}", [P, GT]) for i in range(7)]
        norm2 = sb("norm2", [P, GT])
        norm = sb("norm", [P, NT])
        sd_x = sb("sd_x", [P, GT])
        sd_hi = sb("sd_hi", [P, GT])
        sd_lo = sb("sd_lo", [P, GT])
        inv = sb("inv", [P, GT])
        ninv = sb("ninv", [P, GT])
        root0 = sb("root0", [P, GT])
        at = [0]

        def carve(n):
            at[0] += n
            return raw[:, at[0] - n:at[0]]

        onehotT = [carve(S) for _ in range(2)]
        plainT = [carve(SEL) for _ in range(2)]
        mx = carve(CH)
        onehot = carve(TB * (SEL + 1)).rearrange("p (t q) -> p t q", q=SEL + 1)
        ctxT = carve(SEL)
        xb = [carve(TB * D).rearrange("p (t h) -> p t h", h=D) for _ in range(2)]
        eb = [carve(TB * P).rearrange("p (t h) -> p t h", h=P) for _ in range(2)]
        ecol = [carve(TB) for _ in range(2)]
        xbT = carve(S)
        kT = [carve(S) for _ in range(2)]
        v = [carve(TB * D).rearrange("p (t h) -> p t h", h=D) for _ in range(2)]
        gt_out = carve(S)
        eq_out = carve(S)
        n_gt = carve(TB)
        n_eq = carve(TB)
        rank = carve(TB)
        xqT = carve(SEL)
        qT = carve(SEL)
        qbd = [carve(NH * TOP).rearrange("p (h q) -> p h q", q=TOP) for _ in range(2)]
        prob = carve(CH * S).rearrange("p (c s) -> p c s", s=S)
        nmx = carve(CH)
        den = carve(CH)
        rden = carve(CH)
        pT = carve(TB * NH * TOP).rearrange("p (t r) -> p t r", t=TB)
        picked = carve(NH * TOP).rearrange("p (h q) -> p h q", q=TOP)
        cx = carve(TOP)
        res = carve(D)
        bank = [ctx.enter_context(nc.psum_tensor(f"bank{i}", [P, GN], fp32)) for i in range(8)]
        NH_PS = 3
        h_ps = [[bank[(e * FC + f) % NH_PS] for f in range(FC)] for e in range(E)]
        y_ps = bank[3:5]
        a_ps, t_ps, m_ps = bank[5], bank[6], bank[7]

        ld_x = [sem(f"ld_x{g}") for g in range(NG)]
        ld_rows = sem("ld_rows")
        ld_w1, ld_w2 = ([sem(f"ld_w{w}_{l}") for l in range(L)] for w in (1, 2))
        ld_proj, ld_small, ld_b2 = sem("ld_proj"), sem("ld_small"), sem("ld_b2")
        pool_seq = sem("pool_seq")
        pool_ident = sem("pool_ident")
        pool_eye = sem("pool_eye")
        pool_const = sem("pool_const")
        pool_w2 = sem("pool_w2")
        pool_bias = sem("pool_bias")
        pool_alone = sem("pool_alone")
        pool_sd0 = sem("pool_sd0")
        pool_grp = sem("pool_grp")
        pool_sd = sem("pool_sd")
        pool_root = sem("pool_root")
        pool_xn = sem("pool_xn")
        pool_store = sem("pool_store")
        pool_out = sem("pool_out")
        dve_seq = sem("dve_seq")
        dve_setup = sem("dve_setup")
        dve_var0 = sem("dve_var0")
        dve_rsd0 = sem("dve_rsd0")
        dve_diag = sem("dve_diag")
        dve_brow = sem("dve_brow")
        dve_b2 = sem("dve_b2")
        dve_b1 = sem("dve_b1")
        dve_w1 = sem("dve_w1")
        dve_var = sem("dve_var")
        dve_xhat = sem("dve_xhat")
        dve_xT = sem("dve_xT")
        dve_arg = sem("dve_arg")
        dve_comb = sem("dve_comb")
        dve_combT = sem("dve_combT")
        dve_z = sem("dve_z")
        dve_y = sem("dve_y")
        dve_square = sem("dve_square")
        dve_xn = sem("dve_xn")
        pe_setup = sem("pe_setup")
        pe_b1 = sem("pe_b1")
        pe_xT = sem("pe_xT")
        pe_lg = sem("pe_lg")
        pe_combT = sem("pe_combT")
        pe_z = sem("pe_z")
        pe_h = [sem(f"pe_h{f}") for f in range(FC)]
        pe_y = sem("pe_y")
        act_h = [sem(f"act_h{f}") for f in range(FC)]
        act_th = sem("act_th")
        act_seq = sem("act_seq")
        act_xn0 = sem("act_xn0")
        pool_row = sem("pool_row")
        pe_row = sem("pe_row")
        act_xbT = sem("act_xbT")
        pe_kv = sem("pe_kv")
        act_kv = sem("act_kv")
        dve_onehot = sem("dve_onehot")
        pe_xq = sem("pe_xq")
        dve_xq = sem("dve_xq")
        pe_q = sem("pe_q")
        dve_qbd = sem("dve_qbd")
        pe_sc = sem("pe_sc")
        dve_mx = sem("dve_mx")
        act_exp = sem("act_exp")
        dve_prob = sem("dve_prob")
        pe_pT = sem("pe_pT")
        dve_pT = sem("dve_pT")
        act_pT = sem("act_pT")
        pe_cx = sem("pe_cx")
        dve_cx = sem("dve_cx")
        pe_res = sem("pe_res")
        act_res = sem("act_res")
        pe_out = sem("pe_out")
        dve_out = sem("dve_out")
        dve_final = sem("dve_final")
        st_out = sem("st_out")

        class Own:

            def __init__(self, eng, s):
                self.eng, self.s, self.n = eng, s, 0

            def __call__(self, ins, instead=None):
                if instead is not None:
                    ins.then_inc(instead, 1)
                else:
                    self.n += 1
                    ins.then_inc(self.s, 1)
                return self.n

            def wait(self, n=None):
                n = self.n if n is None else n
                if n > 0:
                    self.eng.wait_ge(self.s, n)

            def clear(self):
                self.wait()
                self.eng.sem_clear(self.s)
                self.n = 0

        def load_w2(eng, l):
            eng.dma_start(w2_raw[:, l].rearrange("p e (c h) -> p e c h", h=D),
                          w2_dram[l].rearrange("e (c p) h -> p e c h", p=P)).then_inc(ld_w2[l], 16)

        def snap(eng, x):
            return x if isinstance(x, int) else eng.snap(x)

        def keys_ahead(eng, l, n, s, last):
            if l >= LX:
                return True, snap(eng, n - (NX - 2)), 1 - s
            return (l == LX - 1 and last and s == 0), 1, 0

        block = ctx.enter_context(nc.Block())

        @block.sync
        def _(sp):
            def load_x(g):
                sp.dma_start(x_in[:, g * GT:(g + 1) * GT, :],
                             x_v[:, g * GT:(g + 1) * GT, :]).then_inc(ld_x[g], 16)

            load_x(0)
            load_x(1)
            sp.dma_start(rows[COL_G:COL_B, :], ln_g.rearrange("l e h -> (l e) h")).then_inc(ld_rows, 16)
            sp.dma_start(rows[COL_B1:COL_QKV, :],
                         b1_dram.rearrange("l e (c p) -> (l e c) p", p=P)).then_inc(ld_rows, 16)

            def load_w1(l):
                sp.dma_start(w1_raw[:, l], w1_dram[l].rearrange("e p f -> p e f")).then_inc(ld_w1[l], 16)

            load_w1(0)
            for k in range(3):
                sp.dma_start(b2[k * E:(k + 1) * E], b2_dram.rearrange("l e h -> e l h")).then_inc(ld_b2, 16)
            for g in range(2, NG):
                load_x(g)
            sp.dma_start(proj[:, 0:3, :], in_proj_w.rearrange("(c p) h -> p c h", p=P)).then_inc(ld_proj, 16)
            sp.dma_start(proj[:, 3, :], out_w).then_inc(ld_proj, 16)
            for l in range(1, L):
                load_w1(l)
            for l in range(1, L):
                load_w2(sp, l)
            with sp.Fori(0, NG - 1) as g:
                sp.wait_ge(pool_out, sp.snap(g + 2))
                sp.dma_start(out_v[:, bass.ds(g * GT, GT), :], x_in[:, bass.ds(g * GT, GT), :]).then_inc(st_out, 16)
            for t in range(GT):
                tile = (NG - 1) * GT + t
                sp.wait_ge(dve_final, t + 1)
                sp.dma_start(out_v[:, tile, :], x_in[:, tile, :]).then_inc(st_out, 16)
            sp.wait_ge(st_out, 16 * (NG - 1 + GT))

        @block.scalar
        def _(act):
            own = Own(act, act_seq)
            act.dma_start(rows[COL_B:COL_B1, :], ln_b.rearrange("l e h -> (l e) h")).then_inc(ld_rows, 16)
            act.dma_start(rows[COL_QKV:COL_OB, :],
                          in_proj_b.rearrange("(c p) -> c p", p=P)).then_inc(ld_rows, 16)
            act.dma_start(rows[COL_OB:NCOL, :], out_b.unsqueeze(0)).then_inc(ld_rows, 16)
            act.dma_start(rw[:, 0:L * E], router_w.rearrange("l h e -> h l e")).then_inc(ld_small, 16)
            act.dma_start(rb[:, 0:L * E],
                          router_b.rearrange("l e -> (l e)").partition_broadcast(P)).then_inc(ld_small, 16)
            load_w2(act, 0)
            for f in range(FC):
                act.sem_inc(act_h[f], 1)

            def first_norm(g1, tile, out=None):
                out = state[:, bass.ds(tile, GT), :] if out is None else out
                act.wait_ge(dve_rsd0, g1)
                xs = x_in[:, bass.ds(tile, GT), :]
                for t in range(GT):
                    own(nc.scalar.activation(x_dev[:, t], xs[:, t], ACT.Identity, bias=nmean0[:, t:t + 1]))
                own.wait()
                for t in range(GT):
                    ins = nc.scalar.activation(out[:, t], x_dev[:, t], ACT.Identity,
                                               scale=rsd0[:, t:t + 1])
                    own(ins, act_xn0) if t == GT - 1 else own(ins)

            def weigh(n2):
                act.wait_ge(dve_arg, n2)
                nc.scalar.activation(th[:], arg[:], ACT.Tanh).then_inc(act_th, 1)

            def keep_xbT(b2_):
                act.wait_ge(pe_row, b2_)
                nc.scalar.copy(xbT[:], t_ps[:, S:2 * S]).then_inc(act_xbT, 1)

            def keep_kv(b2_, s):
                act.wait_ge(pe_kv, b2_)
                nc.scalar.activation(kT[s][:], t_ps[:, 0:S], ACT.Identity,
                                     bias=cols[:, COL_QKV + 1:COL_QKV + 2])
                nc.scalar.copy(v[s][:].rearrange("p t h -> p (t h)"), t_ps[:, S:2 * S]).then_inc(act_kv, 1)

            def keep_res(b1):
                act.wait_ge(pe_res, b1)
                nc.scalar.copy(res[0:SEL, :], a_ps[0:SEL, 0:D]).then_inc(act_res, 1)

            def bring_gelu():
                nc.scalar.activation(warm[:], ones[:, 0:1], ACT.Gelu)

            def exponentials(b1):
                act.wait_ge(dve_mx, b1)
                for c in range(CH):
                    ins = nc.scalar.activation(
                        prob[0:QC, c, :], (a_ps, m_ps)[c // 2][0:QC, (c % 2) * S:(c % 2 + 1) * S], ACT.Exp,
                        bias=nmx[0:QC, c:c + 1], scale=SCALE, accum_out=den[0:QC, c:c + 1])
                ins.then_inc(act_exp, 1)
                bring_gelu()

            def keep_pT(b1):
                act.wait_ge(pe_pT, b1)
                nc.scalar.copy(pT[:, 1, :], m_ps[:, 0:NH * TOP]).then_inc(act_pT, 1)

            def step(l, i, s, last):
                n = l * NG + i * 2 + s
                attend = l >= LX
                ahead, b2_, s2 = keys_ahead(act, l, n, s, last)
                c = [snap(act, n * E + k) for k in range(1, E + 1)]
                n2 = snap(act, n + 2)
                if attend:
                    b1 = snap(act, n - (NX - 1))
                for e in range(E):
                    for f in range(FC):
                        if f == 0:
                            act.wait_ge(pe_y, c[e])
                        act.wait_ge(pe_h[f], c[e])
                        nc.scalar.activation(
                            hid[e % 2][:, f, :], h_ps[e][f][:], ACT.Gelu,
                            bias=bias_l[:, e * FC + f:e * FC + f + 1],
                        ).then_inc(act_h[f], 1)
                    if ahead and e == 0:
                        keep_xbT(b2_)
                    if attend and e == 0:
                        keep_res(b1)
                    if ahead and e == 1:
                        keep_kv(b2_, s2)
                    if attend and e == 2:
                        exponentials(b1)
                    if l == 0 and not last and e == 2:
                        first_norm(snap(act, n + 3), snap(act, n * GT + 2 * GT))
                if attend:
                    keep_pT(b1)
                weigh(n2)

            first_norm(1, 0, grp[0])
            first_norm(2, GT)
            weigh(1)
            for l in range(L):
                act.wait_ge(pool_bias, l + 1)
                own.clear()
                with act.Fori(0, NG // 2 - 1) as i:
                    bring_gelu()
                    for s in range(2):
                        step(l, i, s, last=False)
                        if l == 0:
                            own.clear()
                for s in range(2):
                    step(l, NG // 2 - 1, s, last=True)
            keep_res(B + 1)

        @block.gpsimd
        def _(pool):
            own = Own(pool, pool_seq)

            def select(t, compare, fill, base, pattern, mult):
                return own(nc.gpsimd.affine_select(out=t, in_=t, compare_op=compare, fill=fill, base=base,
                                                   pattern=pattern, channel_multiplier=mult))

            def first_sd(g1):
                pool.wait_ge(dve_var0, g1)
                nc.gpsimd.tensor_tensor(sd0[:], ve0[:], half[:], ALU.pow).then_inc(pool_sd0, 1)

            own(nc.gpsimd.memset(half[:], 0.5))
            own(nc.gpsimd.memset(ident[:], 0.0))
            own(nc.gpsimd.memset(ones[:], 1.0))
            own(nc.gpsimd.memset(eye[:], 1.0))
            own(nc.gpsimd.memset(before4[:], 0.0))
            own(nc.gpsimd.memset(before[:], 0.0))
            own(nc.gpsimd.memset(heads[:], 1.0))
            own(nc.gpsimd.memset(rw[:, L * E:], 0.0))
            own(nc.gpsimd.memset(rb[:, L * E:], 0.0))
            own(nc.gpsimd.memset(in_mid[:], 1.0))
            own(nc.gpsimd.iota(slot[:], pattern=[[1, SEL]], base=0, channel_multiplier=0,
                               allow_small_or_imprecise_dtypes=True))
            own.wait()
            select(ident[:], ALU.not_equal, 1.0, 0, [[-1, P]], 1)
            own.wait()
            pool.sem_inc(pool_ident, 1)
            select(eye[:], ALU.is_equal, 0.0, 0, [[1, L * E], [-1, L * E]], 0)
            own.wait()
            pool.sem_inc(pool_eye, 1)
            first_sd(1)
            select(in_mid[:], ALU.is_ge, 0.0, -E, [[0, 1]], 1)
            select(before4[:], ALU.is_ge, 1.0, 0, [[-1, E], [1, E]], 0)
            select(before[:], ALU.is_ge, 1.0, 0, [[-P, TB], [1, S]], -1)
            select(heads[:], ALU.is_ge, 0.0, 0, [[-HD, NH], [0, TOP]], 1)
            own.wait()
            select(in_mid[:], ALU.is_ge, 0.0, 2 * E - 1, [[0, 1]], -1)
            select(heads[:], ALU.is_ge, 0.0, HD - 1, [[HD, NH], [0, TOP]], -1)
            own.wait()
            pool.sem_inc(pool_const, 1)

            def exact_root(square, count):
                pool.wait_ge(dve_square, count)
                nc.gpsimd.tensor_tensor(root0[:], square[:], half[:], ALU.pow).then_inc(pool_root, 1)

            def keep_xn(g1, tile):
                pool.wait_ge(dve_setup, 1)
                pool.wait_ge(dve_xn, g1)
                nc.gpsimd.tensor_copy(xn_all[:, bass.ds(tile, GT), :], xn[:]).then_inc(pool_xn, 1)

            def take(tile, s):
                nc.gpsimd.tensor_copy(grp[s][:], state[:, bass.ds(tile, GT), :]).then_inc(pool_grp, 1)

            def deviation(n2):
                pool.wait_ge(dve_var, n2)
                nc.gpsimd.tensor_tensor(sd[:], ve[:], half[:], ALU.pow).then_inc(pool_sd, 1)

            def place_w2(l, e):
                if l > 0:
                    pool.wait_ge(pe_y, (l * NG - 1) * E + e + 3)
                pool.wait_ge(ld_w2[l], 16)
                nc.gpsimd.tensor_copy(w2[:, e].rearrange("p c h -> p (c h)"), w2_raw[:, l, e]).then_inc(pool_w2, 1)

            def place_bias(l):
                pool.wait_ge(act_h[FC - 1], l * NG * E + 1)
                pool.wait_ge(dve_b1, 1 if l == 0 else 2)
                nc.gpsimd.tensor_copy(bias_l[:], bias1[:, l * E:(l + 1) * E].rearrange("p e c -> p (e c)")
                                      ).then_inc(pool_bias, 1)

            def output(c6, tile, s):
                pool.wait_ge(dve_y, c6)
                pool.sem_inc(pool_alone, 1)
                xs = x_in[:, bass.ds(tile, GT), :]
                nc.gpsimd.tensor_tensor(xs, xs, grp[s][:], ALU.add).then_inc(pool_out, 1)

            def store(c6, tile, s):
                pool.wait_ge(dve_y, c6)
                pool.sem_inc(pool_alone, 1)
                nc.gpsimd.tensor_copy(state[:, bass.ds(tile, GT), :], grp[s][:]).then_inc(pool_store, 1)

            def bring(row, s):
                nc.gpsimd.tensor_copy(xb[s][:], xn_all[:, bass.ds(row * TB, TB), :])
                nc.gpsimd.tensor_copy(ecol[s][:], norm[:, bass.ds(row * TB, TB)])
                nc.gpsimd.tensor_copy(
                    eb[s][:], norm[:, bass.ds(row * TB, TB)].unsqueeze(2).to_broadcast([P, TB, P])).then_inc(pool_row, 1)

            def step(l, i, s, last):
                n = l * NG + i * 2 + s
                n1, n2 = snap(pool, n + 1), snap(pool, n + 2)
                c6 = snap(pool, n * E + (E + 2))
                end = last and s == 1
                pool.wait_ge(dve_setup, 1)
                pool.wait_ge(pool_store, snap(pool, n + 1) if l < L - 1 else NG * (L - 1) + 1)
                if l == L - 1:
                    pool.wait_ge(dve_setup, 1)
                    pool.wait_ge(pool_out, snap(pool, i * 2 + (s + 1)))
                if l == 0 and not last:
                    pool.wait_ge(act_xn0, n2)
                take(snap(pool, ((i * 2 + (s + 1)) % NG) * GT), 1 - s)
                deviation(n2)
                if l == 0 and not last:
                    first_sd(snap(pool, n + 3))
                if l >= LX:
                    pool.wait_ge(dve_setup, 1)
                    pool.wait_ge(pe_xq, snap(pool, n - (NX - 1)))
                    bring(snap(pool, (n - (NX - 2)) % B), s)
                elif s == 0:
                    exact_root(var, n1)
                else:
                    keep_xn(snap(pool, l * (NG // 2) + (i + 1)), snap(pool, l * (NG // 2 * GT) + i * GT))
                    exact_root(norm2, n1)
                if l == LX - 1 and last and s == 0:
                    bring(1, 1)
                if end and l < L - 1:
                    for e in range(E - 1):
                        if e == E - 2:
                            place_bias(l + 1)
                        place_w2(l + 1, e)
                if l < L - 1:
                    store(c6, snap(pool, (i * 2 + s) * GT), s)
                elif not end:
                    output(c6, snap(pool, (i * 2 + s) * GT), s)
                if end and l < L - 1:
                    place_w2(l + 1, E - 1)

            pool.sem_inc(pool_grp, 1)
            first_sd(2)
            deviation(1)
            place_w2(0, 0)
            place_bias(0)
            for e in range(1, E):
                place_w2(0, e)
            pool.sem_inc(pool_store, 1)
            for l in range(L):
                if l == L - 1:
                    pool.sem_inc(pool_out, 1)
                if l == LX - 1:
                    pool.wait_ge(pool_w2, LX * E)
                    pool.wait_ge(pool_xn, NG // 2)
                    pool.wait_ge(dve_cx, 1)
                    bring(0, 0)
                with pool.Fori(0, NG // 2 - 1) as i:
                    for s in range(2):
                        step(l, i, s, last=False)
                for s in range(2):
                    step(l, NG // 2 - 1, s, last=True)

        @block.vector
        def _(dve):
            V = nc.vector
            own = Own(dve, dve_seq)

            def wide(t, n, m=D):
                return t.unsqueeze(2).to_broadcast([P, n, m])

            def exact_deviation(tile):
                xg = x_in[:, bass.ds(tile, GT), :]
                k = own(V.tensor_reduce(lane[:], xg.rearrange("p t (k l) -> p t l k", l=16), X, ALU.add))
                own.wait(k)
                l4 = lane[:].rearrange("p t (a b c) -> p t a b c", a=2, b=2)
                k = own(V.tensor_tensor(lane8[:], l4[:, :, :, 0], l4[:, :, :, 1], ALU.add))
                own.wait(k)
                k = own(V.tensor_tensor(lane4[:], lane8[:, :, 0], lane8[:, :, 1], ALU.add))
                own.wait(k)
                l2 = lane4[:].rearrange("p t (a b) -> p t a b", b=2)
                k = own(V.tensor_tensor(lane2[:], l2[:, :, :, 0], l2[:, :, :, 1], ALU.add))
                own.wait(k)
                k = own(V.tensor_tensor(mean[:], lane2[:, :, 0], lane2[:, :, 1], ALU.add))
                own.wait(k)
                k = own(V.tensor_scalar(mean[:], mean[:], 1.0 / D, None, ALU.mult))
                own.wait(k)
                own(V.tensor_tensor(dev[:], xg, wide(mean[:], GT), ALU.subtract))

            def exact_variance():
                own.wait()
                own(V.tensor_tensor(rem[:], dev[:], dev[:], ALU.mult))
                windows(vsum[:])
                own.wait()
                own(V.tensor_scalar(var[:], vsum[:], 1.0 / D, EPS, ALU.mult, ALU.add), dve_square)

            def windows(out, signal=None):
                own.wait()
                own(V.tensor_reduce(win[:], rem[:].rearrange("p t (w k) -> p t w k", w=4), X, ALU.add))
                own.wait()
                own(V.tensor_reduce(out, win[:], X, ALU.add), signal)

            def exact_sqrt(out, a, y, t):
                y_hi, y_lo, hh, hl, ll, r, iy = t
                k1 = own(V.tensor_single_scalar(y_hi.bitcast(u32), y.bitcast(u32), HIGH, ALU.bitwise_and))
                own(V.reciprocal(iy, y))
                own.wait(k1)
                k2 = own(V.tensor_tensor(y_lo, y, y_hi, ALU.subtract))
                k3 = own(V.tensor_tensor(hh, y_hi, y_hi, ALU.mult))
                own.wait(k2)
                own(V.tensor_tensor(hl, y_hi, y_lo, ALU.mult))
                own(V.tensor_tensor(ll, y_lo, y_lo, ALU.mult))
                own.wait(k3)
                own(V.tensor_tensor(r, a, hh, ALU.subtract))
                own.wait()
                own(V.scalar_tensor_tensor(hh, hl, -2.0, r, ALU.mult, ALU.add))
                own.wait()
                own(V.tensor_tensor(r, hh, ll, ALU.subtract))
                own.wait()
                own(V.scalar_tensor_tensor(hl, r, 0.5, iy, ALU.mult, ALU.mult))
                own.wait()
                return own(V.tensor_tensor(out, y, hl, ALU.add))

            def exact_root(count):
                dve.wait_ge(pool_root, count)
                k = exact_sqrt(sd_x[:], var[:], root0[:], [t[:] for t in sqs])
                own.wait(k)
                k1 = own(V.tensor_single_scalar(sd_hi[:].bitcast(u32), sd_x[:].bitcast(u32), HIGH, ALU.bitwise_and))
                k2 = own(V.reciprocal(inv[:], sd_x[:]))
                own.wait(k1)
                own(V.tensor_tensor(sd_lo[:], sd_x[:], sd_hi[:], ALU.subtract))
                own.wait(k2)
                own(V.tensor_scalar(ninv[:], inv[:], -1.0, None, ALU.mult))
                k = own(V.tensor_tensor(q0[:], dev[:], wide(inv[:], GT), ALU.mult))
                own.wait(k)
                k = own(V.tensor_single_scalar(q_hi[:].bitcast(u32), q0[:].bitcast(u32), HIGH, ALU.bitwise_and))
                own.wait(k)
                own(V.tensor_tensor(q_lo[:], q0[:], q_hi[:], ALU.subtract))

            def exact_remainder(products):
                last = [None] * GT
                own.wait()
                for k in products:
                    q, sd_part, other = ((q_hi, sd_hi, dev), (q_hi, sd_lo, rem), (q_lo, sd_hi, rem),
                                         (q_lo, sd_lo, rem))[k]
                    for t in range(GT):
                        if last[t] is not None:
                            own.wait(last[t])
                        last[t] = own(V.scalar_tensor_tensor(
                            rem[:, t], q[:, t], sd_part[:, t:t + 1], other[:, t], ALU.mult,
                            ALU.subtract if k == 0 else ALU.add))

            def exact_quotient(g1):
                own.wait()
                for t in range(GT):
                    ins = V.scalar_tensor_tensor(xn[:, t], rem[:, t], ninv[:, t:t + 1], q0[:, t],
                                                 ALU.mult, ALU.add)
                    own(ins, dve_xn) if t == GT - 1 else own(ins)
                dve.wait_ge(dve_xn, g1)
                own(V.tensor_tensor(rem[:], xn[:], xn[:], ALU.mult))
                windows(norm2[:], dve_square)

            def exact_norm(count, tile):
                dve.wait_ge(pool_root, count)
                exact_sqrt(norm[:, bass.ds(tile, GT)], norm2[:], root0[:], [t[:] for t in sqs])

            def place_w1(l, e):
                w1_g = w1_gs[e % 2]
                own(V.tensor_scalar(w1_g[:], w1_raw[:, l, e], cols[:, COL_G + l * E + e:COL_G + l * E + e + 1],
                                    None, ALU.mult))
                own.wait()
                own(V.tensor_copy(w1_hi[:, e], w1_g[:]))
                own.wait()
                own(V.tensor_tensor(w1_lo[:, e], w1_g[:], w1_hi[:, e].bitcast(fp32), ALU.subtract), dve_w1)

            def group_stats(s, n2):
                dve.wait_ge(pool_grp, n2)
                for t in range(GT):
                    own(V.bn_stats(stats[:, t], grp[s][:, t]))
                own.wait()
                for t in range(GT):
                    own(V.bn_aggr(mv[:, t], stats[:, t]))
                own.wait()
                own(V.tensor_scalar(ve[:], mv[:, :, 1], EPS, None, ALU.add), dve_var)

            def normalise(s, n1, n2):
                dve.wait_ge(pool_sd, n2)
                own(V.reciprocal(rsd[:], sd[:]))
                own.wait()
                if n1 is not None:
                    dve.wait_ge(pe_xT, n1)
                for t in range(GT):
                    ins = V.tensor_scalar(xhat[:, t], grp[s][:, t], mv[:, t, 0:1], rsd[:, t:t + 1],
                                          ALU.subtract, ALU.mult)
                    own(ins, dve_xhat) if t == GT - 1 else own(ins)

            def split_xT(s, n2):
                dve.wait_ge(pe_xT, n2)
                own(V.tensor_copy(xT_hi[s][:], t_ps[:]))
                own.wait()
                own(V.tensor_tensor(xT_lo[s][:], t_ps[:], xT_hi[s][:].bitcast(fp32), ALU.subtract), dve_xT)

            def rank_experts(s, n2, col):
                def over(t):
                    return t[:, bass.ds(col, E)].unsqueeze(1).to_broadcast([P, GT, E])

                own(V.tensor_tensor(lg_a[:], over(rw_sum), wide(mv[:, :, 0], GT, E), ALU.mult))
                own.wait()
                own(V.tensor_tensor(lg_a[:], lg_a[:], over(rb), ALU.add))
                dve.wait_ge(pe_lg, n2)
                parts = m_ps[:, 0:GT * 2 * E].rearrange("p (t k e) -> p t e k", k=2, e=E)
                own(V.tensor_reduce(lg[:], parts, X, ALU.add))
                own.wait()
                own(V.tensor_tensor(lg[:], lg[:], wide(sd[:], GT, E), ALU.mult))
                own.wait()
                own(V.tensor_tensor(lg[:], lg[:], lg_a[:], ALU.add))
                own.wait()
                mine = lg[:].unsqueeze(3).to_broadcast([P, GT, E, E])
                other = lg[:].unsqueeze(2).to_broadcast([P, GT, E, E])
                own(V.tensor_tensor(cmp_eq[:], other, mine, ALU.is_equal))
                own(V.tensor_tensor(cmp_gt[:], other, mine, ALU.is_gt))
                own.wait(own.n - 1)
                own(V.tensor_tensor(cmp_eq[:], cmp_eq[:],
                                    before4[:].unsqueeze(1).to_broadcast([P, GT, E, E]), ALU.mult))
                own.wait()
                own(V.tensor_tensor(cmp_gt[:], cmp_gt[:], cmp_eq[:], ALU.add))
                own.wait()
                own(V.tensor_reduce(place[:], cmp_gt[:], X, ALU.add))
                own.wait()
                own(V.tensor_scalar(chosen[:], place[:], K_TOP - 0.5, None, ALU.is_lt))
                own.wait()
                own(V.tensor_tensor(lg_a[:], lg[:], chosen[:], ALU.mult))
                own.wait()
                own(V.tensor_reduce(two[:], lg_a[:], X, ALU.add))
                own.wait()
                own(V.scalar_tensor_tensor(arg[:], wide(two[:], GT, E), -0.5, lg[:], ALU.mult, ALU.add), dve_arg)

            def combine(s, n2):
                dve.wait_ge(act_th, n2)
                own(V.tensor_scalar(th[:], th[:], 0.5, 0.5, ALU.mult, ALU.add))
                own.wait()
                own(V.tensor_tensor(comb[s][:], th[:], chosen[:], ALU.mult))
                own.wait()
                parts = comb_parts[s]
                for k in range(2):
                    own(V.tensor_copy(parts[:, :, k].bitcast(fp32r), comb[s][:]))
                own.wait(own.n - 1)
                own(V.tensor_tensor(parts[:, :, 2], comb[s][:], parts[:, :, 0], ALU.subtract), dve_comb)

            def keep_combT(n2):
                dve.wait_ge(pe_combT, n2)
                own(V.tensor_copy(combT[:], m_ps[0:KB, :]), dve_combT)

            def add_z(s, n1):
                dve.wait_ge(pe_z, n1)
                own(V.tensor_tensor(grp[s][:], m_ps[:].rearrange("p (t h) -> p t h", h=D), grp[s][:],
                                    ALU.add), dve_z)
                own.wait()

            def add_y(s, e, c3):
                dve.wait_ge(pe_y, c3)
                own.wait()
                for t in range(GT):
                    ins = V.scalar_tensor_tensor(grp[s][:, t], y_ps[e % 2][:, t * D:(t + 1) * D],
                                                 comb[s][:, t, e:e + 1], grp[s][:, t], ALU.mult, ALU.add)
                    own(ins, dve_y) if t == GT - 1 else own(ins)

            def rank_tokens(b2_, s):
                dve.wait_ge(act_xbT, b2_)
                for a in range(TB):
                    e_a = ecol[s][:, a:a + 1]
                    own(V.tensor_scalar(gt_out[:], t_ps[:, 0:S], e_a, None, ALU.is_gt, ALU.add,
                                        accum_out=n_gt[:, a:a + 1]))
                    own(V.scalar_tensor_tensor(eq_out[:], t_ps[:, 0:S], e_a, before[:, a], ALU.is_equal,
                                               ALU.mult, accum_out=n_eq[:, a:a + 1]))
                    own.wait()
                own(V.tensor_tensor(rank[:], n_gt[:], n_eq[:], ALU.add))
                own.wait()
                own(V.tensor_scalar(rank[:], rank[:], float(TOP), None, ALU.min))
                own.wait()
                own(V.tensor_tensor(onehot[:, :, 0:SEL], slot[:].unsqueeze(1).to_broadcast([P, TB, SEL]),
                                    wide(rank[:], TB, SEL), ALU.is_equal), dve_onehot)

            def keep_xq(b2_, s):
                dve.wait_ge(pe_xq, b2_)
                own(V.tensor_copy(xqT[:], t_ps[:, 0:SEL]))
                own(V.tensor_copy(plainT[s][:, TOP:SEL], t_ps[:, SEL:SEL + 1]))
                own(V.tensor_copy(onehotT[s][0:SEL, :], t_ps[0:SEL, P:P + S]), dve_xq)

            def spread_q(b2_, s):
                dve.wait_ge(pe_q, b2_)
                own(V.tensor_scalar(qT[:, 0:TOP], t_ps[:, 0:TOP], cols[:, COL_QKV:COL_QKV + 1], None, ALU.add))
                own.wait()
                own(V.tensor_tensor(qbd[s][:], qT[:, 0:TOP].unsqueeze(1).to_broadcast([P, NH, TOP]),
                                    heads[:], ALU.mult), dve_qbd)

            def maxima(b1):
                dve.wait_ge(pe_sc, b1)
                for c, ps in enumerate((a_ps, m_ps)):
                    own(V.tensor_reduce(mx[0:QC, 2 * c:2 * c + 2],
                                        ps[0:QC, :].rearrange("p (c s) -> p c s", s=S), X, ALU.max))
                own.wait()
                own(V.tensor_scalar(nmx[0:QC, :], mx[0:QC, :], -SCALE, None, ALU.mult), dve_mx)

            def probabilities(b1):
                dve.wait_ge(act_exp, b1)
                own(V.reciprocal(rden[0:QC, :], den[0:QC, :]))
                own.wait()
                for c in range(CH):
                    ins = V.tensor_scalar(prob[0:QC, c], prob[0:QC, c], rden[0:QC, c:c + 1], None, ALU.mult)
                    own(ins, dve_prob) if c == CH - 1 else own(ins)

            def keep_pT(b1):
                dve.wait_ge(pe_pT, b1)
                own(V.tensor_copy(pT[:, 0, :], a_ps[:, 0:NH * TOP]), dve_pT)

            def pick_heads(b1):
                dve.wait_ge(pe_cx, b1)
                own(V.tensor_tensor(picked[:], a_ps[:, 0:NH * TOP].rearrange("p (h q) -> p h q", q=TOP),
                                    heads[:], ALU.mult))
                own.wait()
                own(V.tensor_reduce(cx[:], picked[:].rearrange("p h q -> p q h"), X, ALU.add))
                own.wait()
                own(V.tensor_scalar(ctxT[:, 0:TOP], cx[:], cols[:, COL_QKV + 2:COL_QKV + 3], None,
                                    ALU.add), dve_cx)

            def add_attention(b1, tile):
                dve.wait_ge(pe_out, b1)
                own(V.tensor_tensor(x_in[:, bass.ds(tile, TB), :],
                                    a_ps[:, 0:TB * D].rearrange("p (t h) -> p t h", h=D),
                                    x_in[:, bass.ds(tile, TB), :], ALU.add), dve_out)

            def first_variance(tile):
                xs = x_in[:, bass.ds(tile, GT), :]
                for t in range(GT):
                    own(V.bn_stats(stats0[:, t], xs[:, t]))
                own.wait()
                for t in range(GT):
                    own(V.bn_aggr(mv0[:, t], stats0[:, t]))
                own.wait()
                own(V.tensor_scalar(ve0[:], mv0[:, :, 1], EPS, None, ALU.add), dve_var0)

            def first_deviation(g1):
                own(V.tensor_scalar(nmean0[:], mv0[:, :, 0], -1.0, None, ALU.mult))
                own.wait()
                dve.wait_ge(pool_sd0, g1)
                own(V.reciprocal(rsd0[:], sd0[:]), dve_rsd0)

            def bias_as_rows(m1, count):
                dve.wait_ge(pe_b1, count)
                own(V.tensor_copy(bias_rows[0:m1, :], a_ps[0:m1, :]), dve_brow)

            def first_biases(m0, m1, count):
                dve.wait_ge(pe_b1, count)
                own(V.tensor_tensor(bias1[:, m0:m1], a_ps[:, 0:FC * m1].rearrange("p (c m) -> p m c", m=m1)[:, m0:m1],
                                    cols[:, COL_B1 + m0 * FC:COL_B1 + m1 * FC].rearrange("p (m c) -> p m c", c=FC),
                                    ALU.add), dve_b1)

            dve.wait_ge(ld_x[0], 16)
            first_variance(0)
            first_deviation(1)
            dve.wait_ge(pe_setup, 1)
            own(V.tensor_copy(cols[:], t_ps[:, 0:NCOL]))
            own.wait()
            dve.wait_ge(pool_eye, 1)
            own(V.tensor_tensor(ln_b_diag[:], cols[:, COL_B:COL_B1].unsqueeze(2).to_broadcast([P, L * E, L * E]),
                                eye[:], ALU.mult), dve_diag)
            dve.wait_ge(ld_x[1], 16)
            first_variance(GT)
            dve.wait_ge(act_xn0, 1)
            group_stats(0, 1)
            first_deviation(2)
            dve.wait_ge(ld_w1[0], 16)
            place_w1(0, 0)
            normalise(0, None, 1)
            bias_as_rows(E, 1)
            dve.wait_ge(ld_small, 32)
            rw_v = rw[:].rearrange("p (l e) -> p l e", e=E)
            own(V.tensor_copy(rw_parts[:, :, 0], rw_v))
            own.wait()
            own(V.tensor_tensor(rw_parts[:, :, 1], rw_v, rw_parts[:, :, 0].bitcast(fp32), ALU.subtract), dve_setup)
            split_xT(0, 1)
            first_biases(0, E, 2)
            dve.wait_ge(pe_setup, 2)
            own(V.tensor_copy(rw_sum[:], y_ps[0][:, 0:LE1]))
            own.wait()
            rank_experts(0, 1, 0)
            place_w1(0, 1)
            combine(0, 1)
            dve.wait_ge(pool_const, 1)
            dve.wait_ge(ld_b2, 48)
            own(V.tensor_copy(b2_hi.bitcast(fp32r), b2))
            own(V.tensor_scalar(out_mid[:], in_mid[:], -1.0, 1.0, ALU.mult, ALU.add))
            own.wait()
            own(V.tensor_tensor(b2_lo, b2, b2_hi, ALU.subtract))
            own.wait()
            own(V.tensor_scalar(b2_lo, b2_lo, in_mid[:, 0:1], None, ALU.mult))
            own.wait()
            own(V.scalar_tensor_tensor(b2_parts[:], b2_hi, out_mid[:, 0:1], b2_lo,
                                       ALU.mult, ALU.add), dve_b2)
            place_w1(0, 2)
            place_w1(0, 3)
            for g in range(2, NG):
                dve.wait_ge(ld_x[g], 16)
            dve.sem_inc(dve_y, 2)

            def step(l, i, s, last):
                n = l * NG + i * 2 + s
                c = {k: snap(V, n * E + k) for k in range(3, E + 3)}
                n1, n2 = snap(V, n + 1), snap(V, n + 2)
                g_tile = snap(V, l * (NG // 2 * GT) + i * GT)
                attend = l >= LX
                place = last and s == 1 and l < L - 1
                if attend:
                    b1 = snap(V, n - (NX - 1))
                ahead, b2_, s2 = keys_ahead(V, l, n, s, last)
                keep_combT(n1)
                if ahead:
                    rank_tokens(b2_, s2)
                add_z(s, n1)
                if attend:
                    add_attention(b1, snap(V, ((n - (NX - B + 1)) % B) * TB))
                if l == 0 and not last:
                    first_variance(snap(V, n * GT + 2 * GT))
                group_stats(1 - s, n2)
                if place:
                    place_w1(l + 1, 0)
                col = snap(V, ((n + 1) // NG) * E)
                add_y(s, 0, c[3])
                normalise(1 - s, n1, n2)
                if place:
                    place_w1(l + 1, 1)
                if l == 0 and not last:
                    first_deviation(snap(V, n + 3))
                if attend:
                    maxima(b1)
                elif s == 0:
                    exact_deviation(g_tile)
                else:
                    exact_remainder((0, 1))
                add_y(s, 1, c[4])
                split_xT(1 - s, n2)
                if attend:
                    probabilities(b1)
                elif s == 0:
                    exact_variance()
                else:
                    exact_remainder((2, 3))
                    exact_quotient(snap(V, l * (NG // 2) + (i + 1)))
                if ahead:
                    keep_xq(b2_, s2)
                if attend:
                    keep_pT(b1)
                    if place:
                        place_w1(l + 1, 2)
                else:
                    rank_experts(1 - s, n2, col)
                    if s == 0:
                        exact_root(n1)
                add_y(s, 2, c[5])
                if place and attend:
                    place_w1(l + 1, 3)
                if attend:
                    rank_experts(1 - s, n2, col)
                if ahead:
                    spread_q(b2_, s2)
                if attend:
                    pick_heads(b1)
                combine(1 - s, n2)
                if place and not attend:
                    place_w1(l + 1, 2)
                    place_w1(l + 1, 3)
                if not attend and s == 1:
                    exact_norm(n1, g_tile)
                add_y(s, 3, c[6])
                own.clear()

            own.clear()
            for l in range(L):
                if l == LX - 1:
                    dve.wait_ge(pool_w2, E)
                    for t in (onehotT[1], plainT[1], mx):
                        own(V.memset(t[:], 0.0))
                    own.wait()
                    for t in plainT:
                        own(V.tensor_copy(t[:, 0:TOP], cols[:, COL_OB:COL_OB + 1].to_broadcast([P, TOP])))
                    own(V.memset(onehot[:, :, SEL:], 1.0 / S))
                    own(V.memset(ctxT[:], 0.0), dve_cx)
                    dve.wait_ge(dve_cx, 1)
                    own.clear()
                with dve.Fori(0, NG // 2 - 1) as i:
                    for s in range(2):
                        step(l, i, s, last=False)
                if l == 0:
                    bias_as_rows(L * E, 3)
                    first_biases(E, L * E, 4)
                if l == LX - 1:
                    dve.wait_ge(pe_setup, 3)
                    own(V.tensor_copy(projT[:].rearrange("p c h -> p (c h)"), a_ps[:]))
                for s in range(2):
                    if l < L - 1:
                        dve.wait_ge(ld_w1[l + 1], 16)
                    step(l, NG // 2 - 1, s, last=True)
            add_attention(B + 1, (B - 1) * TB)
            dve.wait_ge(dve_out, B + 1)
            for t in range(GT):
                tile = (NG - 1) * GT + t
                own(V.tensor_tensor(x_in[:, tile, :], x_in[:, tile, :], grp[1][:, t], ALU.add), dve_final)

        @block.tensor
        def _(pe):
            T = nc.tensor
            pe.wait_ge(pool_ident, 1)
            pe.wait_ge(ld_rows, 80)
            T.transpose(t_ps[:, 0:NCOL], rows[0:NCOL, :], ident[0:NCOL, 0:NCOL]).then_inc(pe_setup, 1)

            def transpose_x(n2, n1, b2_=None):
                pe.wait_ge(dve_xhat, n2)
                if n1 is not None:
                    pe.wait_ge(dve_xT, n1)
                if b2_ is not None:
                    pe.wait_ge(act_kv, b2_)
                for t in range(GT):
                    ins = T.transpose(t_ps[:, t * P:(t + 1) * P], xhat[:, t], ident[:])
                ins.then_inc(pe_xT, 1)

            def route(s, n2, n1, l, b1=None):
                pe.wait_ge(dve_xT, n2)
                if n1 is not None:
                    pe.wait_ge(dve_z, n1)
                if b1 is not None:
                    pe.wait_ge(act_pT, b1)
                rw_l = rw_parts[:, bass.ds(l, 1)].rearrange("p o k e -> p (o k e)")
                for t in range(GT):
                    o = m_ps[:, t * 2 * E:(t + 1) * 2 * E]
                    hi, lo = (x[s][:, t * P:(t + 1) * P] for x in (xT_hi, xT_lo))
                    T.matmul(o, hi, rw_l, start=True, stop=False)
                    ins = T.matmul(o[:, 0:E], lo, rw_l[:, 0:E], start=False, stop=True)
                ins.then_inc(pe_lg, 1)

            def transpose_comb(s, n2):
                pe.wait_ge(dve_comb, n2)
                for t in range(GT):
                    ins = T.transpose(m_ps[0:KB, t * P:(t + 1) * P],
                                      comb_parts[s][:, t].rearrange("p k e -> p (k e)"), ident[:])
                ins.then_inc(pe_combT, 1)

            def second_bias(n1, l):
                pe.wait_ge(dve_b2, 1)
                pe.wait_ge(dve_combT, n1)
                for t in range(GT):
                    ins = T.matmul(m_ps[:, t * D:(t + 1) * D], combT[:, t * P:(t + 1) * P],
                                   b2_parts[:, l, :], start=True, stop=True)
                ins.then_inc(pe_z, 1)

            def hidden(s, e, c, w):
                pe.wait_ge(dve_w1, w)
                for f in range(FC):
                    before_ = e * FC + f - NH_PS
                    if before_ >= 0:
                        pe.wait_ge(act_h[before_ % FC], c[before_ // FC + 2])
                    else:
                        pe.wait_ge(act_h[max(j for j in range(FC) if h_ps[E - 1][j] is h_ps[e][f])], c[1])
                    hi, lo = (x[:, e, f * P:(f + 1) * P] for x in (w1_hi, w1_lo))
                    T.matmul(h_ps[e][f][:], hi, xT_hi[s][:], start=True, stop=False)
                    T.matmul(h_ps[e][f][:], hi, xT_lo[s][:], start=False, stop=False)
                    T.matmul(h_ps[e][f][:], lo, xT_hi[s][:], start=False, stop=True).then_inc(pe_h[f], 1)

            def outputs(e, c1, c2, w):
                pe.wait_ge(dve_y, c1)
                pe.wait_ge(pool_w2, w)
                for t in range(GT):
                    for f in range(FC):
                        if t == 0:
                            pe.wait_ge(act_h[f], c2)
                        ins = T.matmul(y_ps[e % 2][:, t * D:(t + 1) * D], hid[e % 2][:, f, t * P:(t + 1) * P],
                                       w2[:, e, f], start=(f == 0), stop=(f == FC - 1))
                ins.then_inc(pe_y, 1)

            def row_first(b2_, s):
                pe.wait_ge(pool_row, b2_)
                for a in range(TB):
                    T.transpose(t_ps[:, a * P:(a + 1) * P], eb[s][:, a], ident[:])
                for a in range(TB):
                    ins = T.transpose(t_ps[:, S + a * P:S + (a + 1) * P], xb[s][:, a], ident[:])
                ins.then_inc(pe_row, 1)

            def row_kv(b2_):
                pe.wait_ge(act_xbT, b2_)
                pe.wait_ge(dve_onehot, b2_)
                T.matmul(t_ps[:, 0:S], projT[:, 1], xbT[:], start=True, stop=True)
                for a in range(TB):
                    ins = T.matmul(t_ps[:, S + a * D:S + (a + 1) * D], xbT[:, a * P:(a + 1) * P],
                                   projT[:, 2], start=True, stop=True)
                ins.then_inc(pe_kv, 1)

            def row_select(s):
                for a in range(TB):
                    T.transpose(t_ps[0:SEL, (1 + a) * P:(2 + a) * P], onehot[:, a, 0:SEL], ident[:])
                for a in range(TB):
                    ins = T.matmul(t_ps[:, 0:SEL + 1], xb[s][:, a], onehot[:, a], start=(a == 0), stop=(a == TB - 1))
                ins.then_inc(pe_xq, 1)

            def row_q(b2_):
                pe.wait_ge(dve_xq, b2_)
                T.matmul(t_ps[:, 0:SEL], projT[:, 0], xqT[:], start=True, stop=True).then_inc(pe_q, 1)

            def row_scores(s):
                for c in range(CH):
                    ins = T.matmul(
                        (a_ps, m_ps)[c // 2][0:QC, (c % 2) * S:(c % 2 + 1) * S],
                        qbd[s][:].rearrange("p h q -> p (h q)")[:, c * QC:(c + 1) * QC], kT[s][:],
                        start=True, stop=True)
                ins.then_inc(pe_sc, 1)

            def transpose_prob(b1):
                pe.wait_ge(dve_prob, b1)
                for a, ps in enumerate((a_ps, m_ps)):
                    for c in range(CH):
                        ins = T.transpose(ps[:, c * QC:(c + 1) * QC], prob[0:QC, c, a * P:(a + 1) * P],
                                          ident[0:QC, 0:QC])
                ins.then_inc(pe_pT, 1)

            def contexts(b1, s):
                pe.wait_ge(dve_pT, b1)
                T.matmul(a_ps[:, 0:NH * TOP], v[s][:, 0], pT[:, 0], start=True, stop=False)
                pe.wait_ge(act_pT, b1)
                T.matmul(a_ps[:, 0:NH * TOP], v[s][:, 1], pT[:, 1], start=False, stop=True).then_inc(pe_cx, 1)

            def results(s):
                T.matmul(a_ps[0:SEL, 0:D], plainT[s][:], ident[:], start=True, stop=False)
                T.matmul(a_ps[0:SEL, 0:D], ctxT[:], projT[:, 3], start=False, stop=True).then_inc(pe_res, 1)

            def spread_results(b1, s):
                pe.wait_ge(act_res, b1)
                for a in range(TB):
                    ins = T.matmul(a_ps[:, a * D:(a + 1) * D], onehotT[s][0:SEL, a * P:(a + 1) * P],
                                   res[0:SEL, :], start=True, stop=True)
                ins.then_inc(pe_out, 1)

            def bias_rows_of(m0, m1):
                for m in range(m0, m1):
                    ins = T.matmul(a_ps[0:m1, :], ln_b_diag[:, m, 0:m1], w1_raw[:, m // E, m % E],
                                   start=(m == m0), stop=(m == m1 - 1))
                ins.then_inc(pe_b1, 1)

            def bias_columns(m1, count):
                pe.wait_ge(dve_brow, count)
                for f in range(FC):
                    ins = T.transpose(a_ps[:, f * m1:(f + 1) * m1], bias_rows[0:m1, f * P:(f + 1) * P],
                                      ident[0:m1, 0:m1])
                ins.then_inc(pe_b1, 1)

            def step(l, i, s):
                n = l * NG + i * 2 + s
                attend = l >= LX
                w = [l * E + (e + 1) for e in range(E)]
                c = {k: snap(T, n * E + k) for k in range(1, E + 2)}
                n1, n2 = snap(T, n + 1), snap(T, n + 2)
                if attend:
                    b1 = snap(T, n - (NX - 1))
                ahead, b2_, s2 = keys_ahead(T, l, n, s, l == LX - 1 and isinstance(i, int))
                hidden(s, 0, c, w[0])
                transpose_comb(s, n1)
                if ahead:
                    if attend:
                        pe.wait_ge(dve_qbd, b1)
                    row_first(b2_, s2)
                if attend:
                    pe.wait_ge(dve_cx, b1)
                    results(1 - s)
                hidden(s, 1, c, w[1])
                second_bias(n1, l)
                if attend:
                    spread_results(b1, 1 - s)
                outputs(0, c[1], c[2], w[0])
                if attend:
                    pe.wait_ge(dve_out, b1)
                    pe.wait_ge(dve_z, n1)
                    row_scores(s)
                if ahead:
                    row_kv(b2_)
                hidden(s, 2, c, w[2])
                outputs(1, c[2], c[3], w[1])
                transpose_x(n2, n1, b2_ if ahead else None)
                hidden(s, 3, c, w[3])
                if not attend:
                    route(1 - s, n2, n1, snap(T, (n + 1) // NG))
                if ahead:
                    pe.wait_ge(dve_xT, n2)
                    row_select(s2)
                if attend:
                    transpose_prob(b1)
                outputs(2, c[3], c[4], w[2])
                if attend:
                    route(1 - s, n2, n1, snap(T, (n + 1) // NG), b1)
                if ahead:
                    row_q(b2_)
                if attend:
                    contexts(b1, s)
                outputs(3, c[4], c[5], w[3])

            pe.wait_ge(ld_w1[0], 16)
            pe.wait_ge(dve_diag, 1)
            bias_rows_of(0, E)
            transpose_x(1, None)
            pe.wait_ge(ld_small, 32)
            T.matmul(y_ps[0][:, 0:LE1], ones[:], rw[:], start=True, stop=True).then_inc(pe_setup, 1)
            bias_columns(E, 1)
            pe.wait_ge(pool_const, 1)
            pe.wait_ge(dve_setup, 1)
            route(0, 1, None, 0)
            pe.sem_inc(pe_y, 2)
            for l in range(L):
                with pe.Fori(0, NG // 2 - 1) as i:
                    for s in range(2):
                        step(l, i, s)
                if l == 0:
                    for m in range(1, L):
                        pe.wait_ge(ld_w1[m], 16)
                    pe.wait_ge(dve_b1, 1)
                    bias_rows_of(E, L * E)
                    bias_columns(L * E, 2)
                for s in range(2):
                    step(l, NG // 2 - 1, s)
                if l == 0:
                    pe.wait_ge(ld_proj, 32)
                    pe.wait_ge(dve_b1, 2)
                    for c in range(4):
                        ins = T.transpose(a_ps[:, c * D:(c + 1) * D], proj[:, c, :], ident[:])
                    ins.then_inc(pe_setup, 1)
            pe.wait_ge(dve_cx, B + 1)
            results(1)
            spread_results(B + 1, 1)


_INS = ["L0_attn_x", "L0_attn_in_proj_w", "L0_attn_in_proj_b", "L0_attn_out_w", "L0_attn_out_b",
        "L0_ffn_router_w", "L0_ffn_router_b", "L0_ffn_ln_g", "L0_ffn_ln_b", "L0_ffn_w1", "L0_ffn_b1",
        "L0_ffn_w2", "L0_ffn_b2"]


def kernel(**inputs):
    import numpy as _np
    import concourse.bacc as _bacc
    from concourse import mybir as _mybir
    from concourse.bass_utils import run_bass_kernel_spmd as _run

    nc = _bacc.Bacc("TRN2", target_bir_lowering=False, num_devices=1)
    arrays, args = {}, []
    for name in _INS:
        a = _np.ascontiguousarray(inputs[name])
        arrays[f"in_{name}"] = a
        args.append(nc.dram_tensor(f"in_{name}", a.shape, _mybir.dt.from_np(a.dtype), kind="ExternalInput").ap())
    shape = inputs["L0_attn_x"].shape
    args.append(nc.dram_tensor("out", shape, _mybir.dt.float32, kind="ExternalOutput").ap())
    attention_and_experts_kernel(nc, *args)
    r = _run(nc, [arrays], core_ids=[0])
    return r.results[0]["out"]
```
